# Optimizing a Trainium2 kernel written in Bass

```python
import numpy as np
import jax
import jax.numpy as jnp

def _softmax(x, axis=-1):
    return jax.nn.softmax(x, axis=axis)

def _gelu(x):
    return jax.nn.gelu(x, approximate=True)

def _silu(x):
    return jax.nn.silu(x)

def _sigmoid(x):
    return jax.nn.sigmoid(x)

def _layernorm(x, axis=-1, eps=1e-05):
    m = jnp.mean(x, axis=axis, keepdims=True)
    v = jnp.var(x, axis=axis, keepdims=True)
    return (x - m) / jnp.sqrt(v + eps)

def _scatter_add(tgt, idx, src, axis=0):
    return tgt.at[idx].add(src)

def _segment_sum(src, seg, n):
    return jax.ops.segment_sum(src, seg, n)
kernel_name = 'mk_xattn_ffn_d2_seqx_r4_c0b7c5'

def setup_inputs(seed: int=0):
    np.random.seed(seed)
    _w = jnp.asarray

    def _rec_inputs():
        import jax
        import jax.numpy as jnp
        _rk = jax.random.key(seed)
        x = -0.0003929 + 0.9999 * jax.random.normal(jax.random.fold_in(_rk, 1), (4, 512, 256), jnp.float32)
        _lenS = 512 - jax.random.randint(jax.random.fold_in(_rk, 7), (4,), 0, max(1, 512 // 4) + 1, jnp.int32)
        _lenS2 = 1601 - jax.random.randint(jax.random.fold_in(_rk, 8), (4,), 0, max(1, 1601 // 4) + 1, jnp.int32)
        _ctx_1024P = jax.random.normal(jax.random.fold_in(_rk, 11), (4, 16, 256), jnp.float32)
        _ctx_1024c = jax.random.dirichlet(jax.random.fold_in(_rk, 511), 0.3 * jnp.ones((16,), jnp.float32), (4, 1601))
        _ctx_1024t = jnp.einsum('bsk,bkd->bsd', _ctx_1024c, _ctx_1024P)
        _ctx_1024t = _ctx_1024t * jax.lax.rsqrt(jnp.mean(jnp.square(_ctx_1024t)) + 1e-12) * 0.953939
        ctx_1024 = -3.05549e-07 + 0.0199987 * (_ctx_1024t + 0.3 * jax.random.normal(jax.random.fold_in(_rk, 611), (4, 1601, 256), jnp.float32))
        _validS = jnp.arange(512)[None, :] < _lenS[:, None]
        _validS2 = jnp.arange(1601)[None, :] < _lenS2[:, None]
        _causal = jnp.tril(jnp.ones((512, 512), dtype=bool))
        mask_Bx1x1xS2_bk0 = jnp.logical_not(jnp.broadcast_to(_validS2[:, None, None, :], (4, 1, 1, 1601)))
        return (x, ctx_1024, mask_Bx1x1xS2_bk0)
    x, ctx_1024, mask_Bx1x1xS2_bk0 = _rec_inputs()

    def _L0_xattn_setup():
        import jax, jax.numpy as jnp
        import numpy as np
        E, T, H, F = (8, 512, 256, 1024)
        key = jax.random.key(seed)
        k1, k2, k3 = jax.random.split(key, 3)
        x = jax.random.normal(k1, (E, T, H), dtype=jnp.float32)
        w1 = jax.random.normal(k2, (E, F, H), dtype=jnp.float32) * 0.02
        w2 = jax.random.normal(k3, (E, F, H), dtype=jnp.float32) * 0.02
        return {'x': x, 'w1': w1, 'w2': w2}
    _L0_xattn_all = _L0_xattn_setup()
    _L0_xattn_in = {k: v for k, v in _L0_xattn_all.items() if k in ()}
    del _L0_xattn_all

    def _L0_ffn_setup():
        import jax, jax.numpy as jnp
        import numpy as np
        key = jax.random.key(seed)
        k0, k1, k2, k3 = jax.random.split(key, 4)
        B, S, D, F, E = (8, 512, 256, 512, 8)
        x = jax.random.normal(k0, (B, S, D), dtype=jnp.float32)
        Wg = jax.random.normal(k1, (D, E), dtype=jnp.float32) * 0.02
        W1 = jax.random.normal(k2, (E, D, F), dtype=jnp.float32) * 0.02
        W2 = jax.random.normal(k3, (E, F, D), dtype=jnp.float32) * 0.02
        return {'x': x, 'Wg': Wg, 'W1': W1, 'W2': W2}
    _L0_ffn_all = _L0_ffn_setup()
    _L0_ffn_in = {k: v for k, v in _L0_ffn_all.items() if k in ('Wg', 'W1', 'W2')}
    del _L0_ffn_all

    def _L1_xattn_setup():
        import math
        import jax, jax.numpy as jnp
        import numpy as np
        NUM_BUCKETS = 32
        MAX_DISTANCE = 128
        H = 16
        D_MODEL = 256
        D_K = D_MODEL // H

        def _relative_position_bucket(relative_position):
            nb = NUM_BUCKETS // 2
            buckets = (relative_position > 0).astype(jnp.int32) * nb
            rp = jnp.abs(relative_position)
            max_exact = nb // 2
            is_small = rp < max_exact
            rp_large = max_exact + (jnp.log(jnp.maximum(rp, 1).astype(jnp.float32) / max_exact) / math.log(MAX_DISTANCE / max_exact) * (nb - max_exact)).astype(jnp.int32)
            rp_large = jnp.minimum(rp_large, nb - 1)
            return buckets + jnp.where(is_small, rp, rp_large)
        key = jax.random.key(seed)
        ks = jax.random.split(key, 8)
        B, T_k, T_q = (4, 512, 256)
        std = D_MODEL ** (-0.5)
        inp = {'src': jax.random.normal(ks[0], (B, T_k, D_MODEL), dtype=jnp.float32), 'dst': jax.random.normal(ks[1], (B, T_q, D_MODEL), dtype=jnp.float32), 'mask': jax.random.randint(ks[2], (B, 1, 1, T_k), 0, 2).astype(bool), 'Wq': jax.random.normal(ks[3], (D_MODEL, D_MODEL), dtype=jnp.float32) * std, 'Wk': jax.random.normal(ks[4], (D_MODEL, D_MODEL), dtype=jnp.float32) * std, 'Wv': jax.random.normal(ks[5], (D_MODEL, D_MODEL), dtype=jnp.float32) * std, 'Wo': jax.random.normal(ks[6], (D_MODEL, D_MODEL), dtype=jnp.float32) * std, 'rel_bias': jax.random.normal(ks[7], (H, NUM_BUCKETS), dtype=jnp.float32) * NUM_BUCKETS ** (-0.5)}
        return inp
    _L1_xattn_all = _L1_xattn_setup()
    _L1_xattn_in = {k: v for k, v in _L1_xattn_all.items() if k in ('Wq', 'Wk', 'Wv', 'Wo', 'rel_bias')}
    del _L1_xattn_all

    def _L1_ffn_setup():
        import jax, jax.numpy as jnp
        import numpy as np
        B, S, H = (8, 1024, 256)
        NAV = 128
        E = 8
        F = 2 * H
        key = jax.random.key(seed)
        ks = jax.random.split(key, 12)

        def w(k, shape, fan_in):
            return jax.random.normal(k, shape, dtype=jnp.float32) / np.sqrt(fan_in)
        return {'hidden_states': jax.random.normal(ks[0], (B, S, H), dtype=jnp.float32), 'Wp1': w(ks[1], (H, NAV), H), 'bp1': jnp.zeros((NAV,), jnp.float32), 'Wp2': w(ks[2], (NAV, E), NAV), 'bp2': jnp.zeros((E,), jnp.float32), 'W1': w(ks[3], (E, H, F), H), 'b1': jnp.zeros((E, F), jnp.float32), 'W2': w(ks[4], (E, F, H), F), 'b2': jnp.zeros((E, H), jnp.float32), 'Wo': w(ks[5], (H, H), H), 'bo': jnp.zeros((H,), jnp.float32)}
    _L1_ffn_all = _L1_ffn_setup()
    _L1_ffn_in = {k: v for k, v in _L1_ffn_all.items() if k in ('Wp1', 'bp1', 'Wp2', 'bp2', 'W1', 'b1', 'W2', 'b2', 'Wo', 'bo')}
    del _L1_ffn_all
    return {'x': x, 'ctx_1024': ctx_1024, 'mask_Bx1x1xS2_bk0': mask_Bx1x1xS2_bk0, 'L0_ffn_Wg': _L0_ffn_in['Wg'], 'L0_ffn_W1': _L0_ffn_in['W1'], 'L0_ffn_W2': _L0_ffn_in['W2'], 'L1_xattn_Wq': _L1_xattn_in['Wq'], 'L1_xattn_Wk': _L1_xattn_in['Wk'], 'L1_xattn_Wv': _L1_xattn_in['Wv'], 'L1_xattn_Wo': _L1_xattn_in['Wo'], 'L1_xattn_rel_bias': _L1_xattn_in['rel_bias'], 'L1_ffn_Wp1': _L1_ffn_in['Wp1'], 'L1_ffn_bp1': _L1_ffn_in['bp1'], 'L1_ffn_Wp2': _L1_ffn_in['Wp2'], 'L1_ffn_bp2': _L1_ffn_in['bp2'], 'L1_ffn_W1': _L1_ffn_in['W1'], 'L1_ffn_b1': _L1_ffn_in['b1'], 'L1_ffn_W2': _L1_ffn_in['W2'], 'L1_ffn_b2': _L1_ffn_in['b2'], 'L1_ffn_Wo': _L1_ffn_in['Wo'], 'L1_ffn_bo': _L1_ffn_in['bo']}

def reference(x, ctx_1024, mask_Bx1x1xS2_bk0, L0_ffn_Wg, L0_ffn_W1, L0_ffn_W2, L1_xattn_Wq, L1_xattn_Wk, L1_xattn_Wv, L1_xattn_Wo, L1_xattn_rel_bias, L1_ffn_Wp1, L1_ffn_bp1, L1_ffn_Wp2, L1_ffn_bp2, L1_ffn_W1, L1_ffn_b1, L1_ffn_W2, L1_ffn_b2, L1_ffn_Wo, L1_ffn_bo):
    import jax
    import jax.numpy as jnp

    def _L0_xattn_ref(x, w1, w2):
        import jax, jax.numpy as jnp
        import numpy as np
        E, T, H, F = (8, 512, 256, 1024)
        h = jnp.einsum('eth,efh->etf', x, w1)
        a = jax.nn.gelu(h, approximate=True)
        return jnp.einsum('etf,efh->eth', a, w2)

    def _L0_ffn_ref(x, Wg, W1, W2):
        import jax, jax.numpy as jnp
        import numpy as np
        B, S, D = x.shape
        E = Wg.shape[1]
        T = B * S
        cap = max(1, T // E)
        xt = x.reshape(T, D)
        logits = xt @ Wg
        probs = jax.nn.softmax(logits, axis=-1)
        pT = probs.T
        _, top_idx = jax.lax.top_k(pT, cap)
        sel = jnp.zeros((E, T), dtype=bool).at[jnp.arange(E)[:, None], top_idx].set(True)
        masked = jnp.where(sel, pT, -jnp.inf)
        assigned = sel.any(axis=0)
        tok2exp = jnp.where(assigned, jnp.argmax(masked, axis=0), jnp.argmax(pT, axis=0))
        weights = jnp.take_along_axis(probs, tok2exp[:, None], axis=1)[:, 0]
        out = jnp.zeros_like(xt)
        for e in range(E):
            gate = jnp.where(tok2exp == e, weights, 0.0)
            h = jax.nn.gelu(xt @ W1[e], approximate=False) @ W2[e]
            out = out + gate[:, None] * h
        return out.reshape(B, S, D)

    def _L1_xattn_ref(src, dst, mask, Wq, Wk, Wv, Wo, rel_bias):
        import math
        import jax, jax.numpy as jnp
        import numpy as np
        NUM_BUCKETS = 32
        MAX_DISTANCE = 128
        H = 16
        D_MODEL = 256
        D_K = D_MODEL // H

        def _relative_position_bucket(relative_position):
            nb = NUM_BUCKETS // 2
            buckets = (relative_position > 0).astype(jnp.int32) * nb
            rp = jnp.abs(relative_position)
            max_exact = nb // 2
            is_small = rp < max_exact
            rp_large = max_exact + (jnp.log(jnp.maximum(rp, 1).astype(jnp.float32) / max_exact) / math.log(MAX_DISTANCE / max_exact) * (nb - max_exact)).astype(jnp.int32)
            rp_large = jnp.minimum(rp_large, nb - 1)
            return buckets + jnp.where(is_small, rp, rp_large)
        B, T_k, _ = src.shape
        T_q = dst.shape[1]
        q = (dst @ Wq.T).reshape(B, T_q, H, D_K)
        k = (src @ Wk.T).reshape(B, T_k, H, D_K)
        v = (src @ Wv.T).reshape(B, T_k, H, D_K)
        scores = jnp.einsum('bqhd,bkhd->bhqk', q, k)
        rel_pos = jnp.arange(T_k)[None, :] - jnp.arange(T_q)[:, None]
        rp_bucket = _relative_position_bucket(rel_pos)
        bias = rel_bias[:, rp_bucket]
        scores = scores + bias[None]
        scores = jnp.where(mask, scores, -1000000000.0)
        attn = jax.nn.softmax(scores, axis=-1)
        out = jnp.einsum('bhqk,bkhd->bqhd', attn, v).reshape(B, T_q, H * D_K)
        return out @ Wo.T

    def _L1_ffn_ref(hidden_states, Wp1, bp1, Wp2, bp2, W1, b1, W2, b2, Wo, bo):
        import jax, jax.numpy as jnp
        import numpy as np
        B, S, H = (8, 1024, 256)
        NAV = 128
        E = 8
        F = 2 * H
        last = hidden_states[:, -1, :]
        logits = jax.nn.gelu(last @ Wp1 + bp1, approximate=False) @ Wp2 + bp2
        action_probs = jax.nn.softmax(logits, axis=-1)
        sel = jnp.argmax(action_probs, axis=-1)
        w1 = W1[sel]
        w2 = W2[sel]
        h = jax.nn.gelu(jnp.einsum('bsh,bhf->bsf', hidden_states, w1) + b1[sel][:, None, :], approximate=False)
        reasoned = jnp.einsum('bsf,bfh->bsh', h, w2) + b2[sel][:, None, :]
        out = reasoned @ Wo + bo
        return hidden_states + 0.3 * out
    x = x + _L0_xattn_ref(_layernorm(x, axis=-1), ctx_1024, ctx_1024)
    x = x + _L0_ffn_ref(_layernorm(x, axis=-1), L0_ffn_Wg, L0_ffn_W1, L0_ffn_W2)
    x = x + _L1_xattn_ref(ctx_1024, _layernorm(x, axis=-1), mask_Bx1x1xS2_bk0, L1_xattn_Wq, L1_xattn_Wk, L1_xattn_Wv, L1_xattn_Wo, L1_xattn_rel_bias)
    x = x + _L1_ffn_ref(_layernorm(x, axis=-1), L1_ffn_Wp1, L1_ffn_bp1, L1_ffn_Wp2, L1_ffn_bp2, L1_ffn_W1, L1_ffn_b1, L1_ffn_W2, L1_ffn_b2, L1_ffn_Wo, L1_ffn_bo)
    return x

_drawn_inputs = setup_inputs


def setup_inputs(seed=0):
    import zlib

    import numpy as np

    out = dict(_drawn_inputs(seed))
    spreads = {'L1_ffn_bp1': (0.0, 0.1),
     'L1_ffn_bp2': (0.0, 0.1),
     'L1_ffn_b1': (0.0, 0.8),
     'L1_ffn_b2': (0.0, 0.8),
     'L1_ffn_bo': (0.0, 0.8)}
    factors = {'L0_ffn_Wg': 7.936,
     'L0_ffn_W1': 7.638,
     'L0_ffn_W2': 7.486,
     'L1_xattn_Wq': 8.0,
     'L1_xattn_Wk': 8.0,
     'L1_xattn_Wv': 8.0,
     'L1_xattn_Wo': 8.0,
     'L1_xattn_rel_bias': 8.0}
    for name, (base, spread) in spreads.items():
        noise = np.random.default_rng([zlib.crc32(name.encode()), seed]).standard_normal(out[name].shape)
        drawn = base * np.exp(spread * noise) if base else spread * noise
        out[name] = jnp.asarray(drawn.astype(out[name].dtype))
    for name, factor in factors.items():
        out[name] = (out[name] * factor).astype(out[name].dtype)
    return out
```

```python
from contextlib import ExitStack
import math

import numpy as np
import concourse.bass as bass
from concourse import mybir
from concourse.alu_op_type import AluOpType as ALU

ACT = mybir.ActivationFunctionType
AX = mybir.AxisListType
F32 = mybir.dt.float32
BF16 = mybir.dt.bfloat16
I32 = mybir.dt.int32
U32 = mybir.dt.uint32
U8 = mybir.dt.uint8

P = 128
B, S, D = 4, 512, 256
L = 1601
T = B * S
NT = T // P
TB = S // P
KC = D // P
NF = -(-L // P)
E, F = 8, 512
FC = F // P
CAP = T // E
NBLK = 24
PAIRS = NBLK // 2
H, DK = 16, 16
CH = 512
NC = -(-L // CH)
LP = NC * CH
CT = CH // P
HG = 4
NG = H // HG
VW = 32
TERMS = 6
KR = TERMS * DK
ROW_MASK = KR
ROW_MAX = KR + 1
KROWS = KR + 4
BUCKETS, MAX_DISTANCE = 32, 128
NY = LP + S
HW_ = S + CH - P
NEG = -1.0e30
EPS = 1e-5
RSQRT_GUESS, NEWTON = 0x5F3759DF, 4
NAV = 128
SEARCH_BITS = 3
ROUNDS = 30 // SEARCH_BITS
CAND = 2 ** SEARCH_BITS - 1


def shape_constants():
    eye = np.eye(P, dtype=np.float32)
    tri = np.triu(np.ones((P, P), np.float32), 1)
    ones = np.ones((P, P), np.float32)
    em8 = np.tile(np.arange(E, dtype=np.float32) - E, (P, 1))
    jt = np.tile(np.arange(NT, dtype=np.float32) * P, (P, 1))
    jb = np.tile(np.arange(NBLK, dtype=np.float32), (P, 1))
    steps = np.zeros((P, ROUNDS), np.float32)
    for r in range(ROUNDS):
        steps[:, r] = 2.0 ** (30 - SEARCH_BITS * (r + 1))
    blk = np.zeros((P, 64), np.float32)
    for i in range(B * NC):
        blk[i, (i // NC) * NC:(i // NC + 1) * NC] = 1.0
        blk[i, 16 + i // NC] = 1.0
        blk[i, 32] = i // NC
        blk[i, 33] = i % NC
    lists = np.zeros((P, 48), np.float32)
    lists[:, 0:16] = np.arange(16) // NC
    lists[:, 16:32] = np.arange(16) % NC
    lists[:, 32:48] = np.arange(16) + 1
    f32 = np.concatenate([eye, tri, ones, em8, jt, jb, steps, blk, lists], axis=1)
    cand = np.zeros((P, ROUNDS * CAND), np.int32)
    for r in range(ROUNDS):
        for c in range(CAND):
            cand[:, r * CAND + c] = (c + 1) << (30 - SEARCH_BITS * (r + 1))
    real = np.zeros((B * NC, CH), np.float32)
    for i in range(B * NC):
        real[i] = (np.arange(CH) + CH * (i % NC)) < L
    rel = (L - 1) - np.arange(NY)
    rp = np.abs(rel)
    half, exact = BUCKETS // 2, BUCKETS // 4
    large = exact + (np.log(np.maximum(rp, 1).astype(np.float32) / np.float32(exact))
                     / np.float32(math.log(MAX_DISTANCE / exact)) * np.float32(half - exact)).astype(np.int32)
    bucket = np.where(rel > 0, half, 0) + np.where(rp < exact, rp, np.minimum(large, half - 1))
    hot = np.zeros((BUCKETS, NY), np.float32)
    hot[bucket, np.arange(NY)] += 1.0
    hot[BUCKETS - 1] -= 1.0
    return {"c_f32": f32, "c_cand": cand, "c_real": real, "c_hot": hot}


C_EYE, C_TRI, C_ONES, C_EM8 = 0, P, 2 * P, 3 * P
C_JT = C_EM8 + E
C_JB = C_JT + NT
C_STEP = C_JB + NBLK
C_BLK = C_STEP + ROUNDS
C_LIST = C_BLK + 64
C_END = C_LIST + 48


class Chain:

    def __init__(self, sem, base=0):
        self.sem, self.n, self.base = sem, 0, base

    def add(self, ins):
        self.n += 1
        ins.then_inc(self.sem, 1)

    def settle(self, eng):
        eng.wait_ge(self.sem, self.base + self.n)

    def step(self, eng, ins):
        self.add(ins)
        self.settle(eng)


def build(nc, a):
    with ExitStack() as ctx:
        def sb(name, shape, dt):
            return ctx.enter_context(nc.sbuf_tensor(name, shape, dt))

        def sem(name):
            return ctx.enter_context(nc.semaphore(name))

        def dram(name, shape, dt):
            return nc.dram_tensor(name, shape, dt, kind="Internal").ap()

        xs_d = dram("xs_sorted", [NBLK * P, D], F32)
        ys_d = dram("ys_sorted", [NBLK * P, D], F32)
        q_d = dram("q_parts", [3, D, T], BF16)
        k_d = dram("k_parts", [3, D, CH], BF16)
        mask_d = dram("mask_rows", [B * NC, CH], BF16)
        dist_d = dram("bias_by_distance", [B, H, NY], F32)

        x_tok = sb("x_tok", [P, NT, D], F32)
        xn = sb("xn", [P, NT, D], F32)
        xnT = sb("xnT", [P, KC, T], F32)
        cst = sb("cst", [P, C_END], F32)
        cand_c = sb("cand_c", [P, ROUNDS * CAND], I32)
        eye_b = sb("eye_b", [P, P], BF16)
        tri_b = sb("tri_b", [P, P], BF16)
        ones_b = sb("ones_b", [P, P], BF16)
        eye = cst[:, C_EYE:C_EYE + P]
        wq = sb("wq", [P, KC, D], F32)
        wk = sb("wk", [P, KC, D], F32)
        wv = sb("wv", [P, KC, D], F32)
        wo = sb("wo", [P, KC, D], F32)
        wg = sb("wg", [P, KC, E], F32)
        relb = sb("relb", [BUCKETS, H], F32)
        lg = sb("router_logits", [P, NT, E], F32)
        zero_t = sb("zero_tile_s", [P, D], F32)
        stats = sb("stats", [P, TB, 6], F32)
        mv = sb("mv", [P, TB, 2], F32)
        rstd = sb("rstd", [P, TB], F32)
        vare = sb("var_eps", [P, TB], F32)
        rsq = sb("root_squared", [P, TB], F32)
        a128 = sb("a128", [P, B], F32)
        maskw = sb("maskw", [B * NC, 4, CH], F32)
        mask4 = sb("mask4", [B * NC, CH // 4], I32)
        mrow_b = sb("mrow_b", [B * NC, CH], BF16)
        msm = sb("msm", [B * NC, 8], F32)
        lst = sb("lst", [1, 8, 16], F32)
        lst2 = sb("lst2", [1, 16, 16], F32)
        lst3 = sb("lst3", [1, 16, 16], F32)
        lst_i = sb("lst_i", [1, 40], I32)

        A_MAX = 32768
        arena = sb("arena", [P, A_MAX], F32)
        at = [0]

        def view(shape, dt=F32, off=None):
            n = int(np.prod(shape))
            words = n if dt in (F32, I32, U32) else -(-n // 2)
            o = at[0] if off is None else off
            at[0] = o + words
            assert at[0] <= A_MAX, at[0]
            v = arena[:, o:o + words]
            if dt != F32:
                v = v.bitcast(dt)[:, 0:n]
            if len(shape) > 1:
                names = "abcd"[:len(shape)]
                v = v.rearrange(f"p ({' '.join(names)}) -> p {' '.join(names)}",
                                **{k: s for k, s in zip(names[1:], shape[1:])})
            return v

        ctxT_s = view([2, KC, NF * P])
        ctxN_s = view([2, NF, D])
        hid = view([4, S])
        part1_end = at[0]
        w1_s = view([E, KC, F])
        w2_s = view([E, FC, D])
        at[0] = 0
        pr = view([NT, E]); sel = view([NT, E]); gt = view([NT, E], BF16)
        t_a = view([NT, E]); t_b = view([NT, E])
        hot_b = view([NT, E], BF16); eq_b = view([NT, E], BF16)
        ge_b = view([CAND, NT, E], BF16)
        cand = view([CAND, E], I32); cur = view([E], I32); npass = view([CAND, E]); nsum = view([E]); ninc = view([E], I32)
        r16 = view([NT]); gate = view([NT]); asg = view([NT])
        need = view([E]); nb = view([E]); cb = view([E]); base_s = view([E]); ones8 = view([E]); nbw = view([E, NT])
        slot_i = view([NT], I32)
        be = view([NBLK]); be_w = view([NBLK, E]); be_i = view([NBLK], I32)
        xsb = view([2, D]); xsT = view([2, KC, P]); hexp = view([2, F]); hexpT = view([2, FC, P])
        y_s = view([2, D]); yg = view([NT, D])
        assert at[0] <= part1_end, (at[0], part1_end)
        at[0] = 0
        qf = view([S]); qr = view([S]); qp = view([3, KC, S], BF16)
        ctx_c = view([KC, CH])
        kp = view([3, KC, CH], BF16); kf = view([KC, CH])
        q_at = at[0]
        Q = view([H, S], BF16); K = view([H, CH], BF16)
        v_at = at[0]
        V = view([CT, H, VW])
        pexp = view([4, 2, S])
        mrow = view([S], BF16)
        cmax = view([H, TB]); nm = view([H, TB]); nmr = view([H, TB])
        nmb = view([TB, P // H, H], BF16)
        m_run = view([B, H * TB]); m_new = view([H * TB]); dif = view([2, H * TB]); scl = view([2, H * TB])
        acc = view([B, TB, H, DK + 1]); tmp = view([TB, HG, DK + 1]); oT = view([2, S])
        Hk = view([HG, HW_])
        rl = view([NT, H])
        at[0] = q_at
        hot_s = view([NY]); dist_s = view([NY]); dist_g = view([NY])
        assert at[0] <= v_at
        at[0] = 0
        p_w1 = view([B, KC, F]); p_w2 = view([B, FC, D]); p_b1 = view([B, FC]); p_b2 = view([B, KC])
        wp1 = view([KC, NAV]); wp2 = view([E]); bp1 = view([1]); bp2 = view([E])
        wof = view([KC, D]); bo_s = view([D])
        nav = view([B]); al = view([8, E]); sel_i = view([4], I32)
        hT = view([2, FC, S]); rT = view([2, KC, S]); base4 = view([NT, D]); o_s = view([NT, D])

        ps = ctx.enter_context(nc.psum_tensor("ps", [P, 8, 512], F32))

        s_const = sem("const_loaded")
        s_x = [sem(f"x_loaded{b}") for b in range(B)]
        s_ctxT = [sem(f"ctxT_loaded{i}") for i in range(2)]
        s_ctxN = [sem(f"ctxN_loaded{i}") for i in range(2)]
        s_wts = sem("weights_loaded")
        s_w12 = sem("expert_weights_loaded")
        s_bconst = sem("bf16_constants")
        s_dv = sem("vector_steps")
        s_ln = sem("layer_norm_done")
        s_tpr = sem("transposed")
        s_tpf = sem("transpose_taken")
        s_h = sem("hidden_product")
        s_a = sem("hidden_activated")
        s_mm2 = sem("hidden_used")
        s_res = sem("residual_added")
        s_soft = sem("router_shifted")
        s_exp8 = sem("router_exp")
        s_ge = sem("candidates_compared")
        s_cnt = sem("candidates_counted")
        s_gq = sem("router_masks")
        s_gp = sem("router_prefixes")
        s_slot = sem("slots_known")
        s_zero = sem("slots_zeroed")
        s_zt = sem("zero_tile")
        s_scat = sem("tokens_scattered")
        s_xsb = sem("block_loaded")
        s_xsTr = sem("block_transposed")
        s_xsT = sem("block_transpose_taken")
        s_eh = sem("expert_hidden")
        s_ea = sem("expert_activated")
        s_et = sem("expert_hidden_transposed")
        s_etc = sem("expert_transpose_taken")
        s_ey = sem("expert_answer")
        s_eyc = sem("expert_answer_taken")
        s_ys = sem("answers_stored")
        s_gat = sem("answers_gathered")
        s_mask = sem("mask_loaded")
        s_mk = sem("mask_any")
        s_mkp = sem("mask_any_by_batch")
        s_mk2 = sem("mask_active")
        s_lrow = sem("active_row")
        s_list = sem("chunk_list")
        s_mrow = sem("mask_row_made")
        s_mst = sem("mask_rows_stored")
        s_dp = sem("distance_product")
        s_dpc = sem("distance_taken")
        s_dst = sem("distances_made")
        s_dstore = sem("distances_stored")
        s_hot = sem("distance_table_loaded")
        s_init3 = sem("attention_buffers_set")
        s_q = sem("q_product")
        s_qp = sem("q_parts_made")
        s_qst = sem("q_parts_stored")
        s_cc = sem("chunk_loaded")
        s_kpr = sem("k_product")
        s_vpr = sem("v_product")
        s_k1 = sem("k_first_part")
        s_kp = sem("k_parts_made")
        s_kst = sem("k_parts_stored")
        s_vt = sem("v_taken")
        s_kq = sem("k_q_rows_loaded")
        s_hk = sem("distance_window_loaded")
        s_dvr = sem("vector_steps_of_a_round")
        s_dvm = sem("chunk_weighted")
        s_rows = sem("constant_rows_set")
        s_dv3 = sem("vector_steps_of_a_chunk")
        s_dtake = sem("distance_buffers_free")
        s_sc = sem("scores_for_max")
        s_scu = sem("scores_for_max_taken")
        s_nm = sem("max_split")
        s_nmt = sem("max_transposed")
        s_nmc = sem("max_rows_made")
        s_mr = sem("max_rows_loaded")
        s_st = sem("scores")
        s_pe = sem("probs")
        s_pv = sem("probs_used")
        s_oc = sem("values_taken")
        s_ot = sem("values_transposed")
        s_ou = sem("values_merged")
        s_wgt = sem("merge_weights_shifted")
        s_wge = sem("merge_weights")
        s_acc_f = sem("attention_normalised")
        s_pj = sem("projected")
        s_w4 = sem("part4_weights_loaded")
        s_nv = sem("router4_product")
        s_nva = sem("router4_activated")
        s_nl = sem("router4_logits")
        s_l4 = sem("router4_shifted")
        s_e4 = sem("router4_exp")
        s_sel = sem("expert4_known")
        s_pw = [sem(f"expert4_loaded{b}") for b in range(B)]
        s_p4 = sem("part4_hidden")
        s_p4a = sem("part4_activated")
        s_p4u = sem("part4_hidden_used")
        s_rt = sem("part4_reasoned")
        s_rtc = sem("part4_reasoned_taken")
        s_po = sem("part4_out")
        s_fo = sem("final_rows")
        s_base = sem("final_base")
        s_out = sem("rows_stored")

        def per(i, k):
            return i * k

        block = ctx.enter_context(nc.Block())

        @block.sync
        def _(sp):
            sp.dma_start(cst[:, :], a["c_f32"]).then_inc(s_const, 16)
            sp.dma_start(x_tok[:, 0:TB, :], a["x"][0:S, :].rearrange("(t p) d -> p t d", p=P)).then_inc(s_x[0], 16)

            def load_ctx(b):
                if b >= 2:
                    sp.wait_ge(s_mm2, NF * (b - 1))
                sp.dma_start(ctxT_s[:, b % 2, :, :], a["ctxT"][b].rearrange("(k p) n -> p k n", p=P)[:, :, 0:NF * P]).then_inc(s_ctxT[b % 2], 16)
                sp.dma_start(ctxN_s[:, b % 2, :, :], a["ctxN"][b].rearrange("(f p) d -> p f d", p=P)).then_inc(s_ctxN[b % 2], 16)

            load_ctx(0)
            for b in range(1, B):
                sp.dma_start(x_tok[:, TB * b:TB * b + TB, :],
                             a["x"][S * b:S * b + S, :].rearrange("(t p) d -> p t d", p=P)).then_inc(s_x[b], 16)
            sp.dma_start(cand_c[:, :], a["c_cand"]).then_inc(s_const, 16)
            sp.dma_start(wg[:, :, :], a["Wg"].rearrange("(k p) e -> p k e", p=P)).then_inc(s_wts, 16)
            load_ctx(1)
            sp.dma_start(mask4[:, :], a["mask"]).then_inc(s_mask, 16)
            sp.dma_start(maskw[:, 0, :], a["c_real"]).then_inc(s_mask, 16)
            sp.dma_start(relb[:, :], a["rel_biasT"]).then_inc(s_mask, 16)
            for w, name in ((wq, "WqT"), (wk, "WkT"), (wv, "WvT"), (wo, "WoT")):
                sp.dma_start(w[:, :, :], a[name].rearrange("(k p) n -> p k n", p=P)).then_inc(s_wts, 16)
            for e in range(E):
                sp.dma_start(w1_s[:, e, :, :], a["W1"][e].rearrange("(k p) f -> p k f", p=P)).then_inc(s_w12, 16)
                sp.dma_start(w2_s[:, e, :, :], a["W2"][e].rearrange("(f p) d -> p f d", p=P)).then_inc(s_w12, 16)
            load_ctx(2)
            load_ctx(3)
            sp.wait_ge(s_mrow, 1)
            sp.dma_start(mask_d, mrow_b[:, :]).then_inc(s_mst, 16)
            sp.wait_ge(s_zt, 1)
            sp.dma_start(xs_d.rearrange("(j p) d -> p j d", p=P),
                         zero_t[:, :].unsqueeze(1).broadcast_to([P, NBLK, D])).then_inc(s_zero, 16)
            sp.wait_ge(s_scat, 16 * NT)

            def load_block(i):
                sp.dma_start(xsb[:, :, :], xs_d.rearrange("(i j p) d -> i p j d", p=P, j=2)[i]).then_inc(s_xsb, 16)

            load_block(0)
            with sp.Fori(0, PAIRS - 1) as i:
                sp.wait_ge(s_xsTr, i * 2 + 2)
                sp.dma_start(xsb[:, :, :], xs_d.rearrange("(i j p) d -> i p j d", p=P, j=2)[bass.ds(i + 1, 1)]
                             .rearrange("i p j d -> (i p) j d")).then_inc(s_xsb, 16)
                sp.wait_ge(s_eyc, i * 2 + 2)
                sp.dma_start(ys_d.rearrange("(i j p) d -> i p j d", p=P, j=2)[bass.ds(i, 1)]
                             .rearrange("i p j d -> (i p) j d"), y_s[:, :, :]).then_inc(s_ys, 16)
            sp.wait_ge(s_eyc, 2 * PAIRS)
            sp.dma_start(ys_d.rearrange("(i j p) d -> i p j d", p=P, j=2)[PAIRS - 1], y_s[:, :, :]).then_inc(s_ys, 16)
            sp.wait_ge(s_init3, 1)
            sp.dma_start(hot_s[0:BUCKETS, :], a["c_hot"]).then_inc(s_hot, 16)
            for b in range(B):
                sp.wait_ge(s_dst, b + 1)
                sp.dma_start(dist_d[b], dist_g[0:H, :]).then_inc(s_dstore, 16)
            for b in range(B):
                sp.wait_ge(s_qp, b + 1)
                for h in range(KC):
                    sp.dma_start(q_d.rearrange("t (k p) n -> p t k n", p=P)[:, :, h, b * S:b * S + S],
                                 qp[:, :, h, :]).then_inc(s_qst, 16)
            sp.wait_ge(s_list, 1)
            n = sp.value_load(lst_i[0:1, 32:33], min_val=1, max_val=B * NC)
            sp.wait_ge(s_rows, 1)
            sp.wait_ge(s_qst, 16 * KC * B)
            sp.wait_ge(s_mst, 16)
            sp.wait_ge(s_dstore, 16 * B)
            with sp.Fori(0, n) as i:
                bi = sp.value_load(lst_i[0:1, bass.ds(i, 1)], min_val=0, max_val=B - 1)
                ci = sp.value_load(lst_i[0:1, bass.ds(i + 16, 1)], min_val=0, max_val=NC - 1)
                sp.wait_ge(s_vpr, i)
                sp.dma_start(ctx_c[:, :, :], a["ctxT"][bass.ds(bi, 1), :, bass.ds(ci * CH, CH)]
                             .rearrange("b (k p) n -> p (b k) n", p=P)).then_inc(s_cc, 16)
                sp.wait_ge(s_pv, i * (NG * CT))
                qv = q_d[:, :, bass.ds(bi * S, S)].rearrange("t (h d) n -> t d h n", d=DK)
                for r, part, reps in ((0, 0, 3), (3, 1, 2), (5, 2, 1)):
                    for k in range(reps):
                        sp.dma_start(Q[(r + k) * DK:(r + k + 1) * DK, :, :], qv[part]).then_inc(s_kq, 16)
                sp.dma_start(K[ROW_MASK:ROW_MASK + 1, :, :],
                             mask_d[bass.ds(bi * NC + ci, 1), :].unsqueeze(1).broadcast_to([1, H, CH])).then_inc(s_kq, 16)
                sp.wait_ge(s_kp, i + 1)
                for h in range(KC):
                    sp.dma_start(k_d.rearrange("t (k p) n -> p t k n", p=P)[:, :, h, :], kp[:, :, h, :]).then_inc(s_kst, 16)
                sp.wait_ge(s_kst, (i + 1) * (16 * KC))
                kv = k_d.rearrange("t (h d) n -> t d h n", d=DK)
                for r, part in enumerate((0, 1, 2, 0, 1, 0)):
                    sp.dma_start(K[r * DK:(r + 1) * DK, :, :], kv[part]).then_inc(s_kq, 16)
                dv = bass.AP(dist_d.tensor, 0, [[H * NY, B], [NY, H], [1, P], [1, NY - P + 1]])

                def window(g):
                    sp.dma_start(Hk[:, :, :], dv[bass.ds(bi, 1), HG * g:HG * g + HG, :, bass.ds(ci * CH, HW_)]
                                 .rearrange("b h k x -> k (b h) x")).then_inc(s_hk, 16)

                with sp.If(ci > 0):
                    for g in range(NG):
                        sp.wait_ge(s_scu, i * (H * TB // 2) + g * (HG * TB // 2))
                        window(g)
                with sp.Else():
                    sp.sem_inc(s_hk, 16 * NG)
                sp.wait_ge(s_nmc, i + 1)
                for t in range(3):
                    sp.dma_start(Q[ROW_MAX + t:ROW_MAX + t + 1, :, :], mrow[t * H:(t + 1) * H, :]).then_inc(s_mr, 16)
                with sp.If(ci > 0):
                    for g in range(NG):
                        sp.wait_ge(s_pv, i * (NG * CT) + g * CT)
                        window(g)
                with sp.Else():
                    sp.sem_inc(s_hk, 16 * NG)
            sp.wait_ge(s_acc_f, B)
            sp.dma_start(wp1[:, :, :], a["Wp1"].rearrange("(k p) n -> p k n", p=P)).then_inc(s_w4, 16)
            sp.dma_start(wp2[:, :], a["Wp2"]).then_inc(s_w4, 16)
            sp.dma_start(bp1[:, :], a["bp1"].unsqueeze(1)).then_inc(s_w4, 16)
            sp.dma_start(bp2[0:B, :], a["bp2"].unsqueeze(0).broadcast_to([B, E])).then_inc(s_w4, 16)
            sp.dma_start(wof[:, :, :], a["Wof"].rearrange("(k p) n -> p k n", p=P)).then_inc(s_w4, 16)
            sp.dma_start(bo_s[:, :], a["bo"].unsqueeze(0).broadcast_to([P, D])).then_inc(s_w4, 16)
            sp.wait_ge(s_sel, 1)
            for b in range(B):
                e = sp.value_load(sel_i[b:b + 1, 0:1], min_val=0, max_val=E - 1)
                sp.dma_start(p_w1[:, b, :, :], a["pW1"][bass.ds(e, 1)].rearrange("e (k p) f -> p (e k) f", p=P)).then_inc(s_pw[b], 16)
                sp.dma_start(p_w2[:, b, :, :], a["pW2"][bass.ds(e, 1)].rearrange("e (f p) d -> p (e f) d", p=P)).then_inc(s_pw[b], 16)
                sp.dma_start(p_b1[:, b, :], a["pb1"][bass.ds(e, 1)].rearrange("e (f p) -> p (e f)", p=P),
                             allow_slow_non_contiguous=True).then_inc(s_pw[b], 16)
                sp.dma_start(p_b2[:, b, :], a["pb2"][bass.ds(e, 1)].rearrange("e (k p) -> p (e k)", p=P),
                             allow_slow_non_contiguous=True).then_inc(s_pw[b], 16)
            for b in range(B):
                sp.wait_ge(s_fo, b + 1)
                sp.dma_start(a["out"][S * b:S * b + S, :].rearrange("(t p) d -> p t d", p=P),
                             o_s[:, TB * b:TB * b + TB, :]).then_inc(s_out, 16)
            sp.wait_ge(s_out, 16 * B)

        @block.tensor
        def _(pe):
            tp = [0]

            def tp_bank():
                if tp[0] >= 2:
                    pe.wait_ge(s_tpf, tp[0] - 1)
                bank = 6 + tp[0] % 2
                tp[0] += 1
                return ps[:, bank, :]

            def transposes(src, b):
                for k in range(KC):
                    o = tp_bank()
                    for t in range(TB):
                        ins = pe.transpose(o[:, t * P:t * P + P], src[:, TB * b + t, k * P:k * P + P], eye)
                    ins.then_inc(s_tpr, 1)

            pe.wait_ge(s_bconst, 1)
            for b in range(2):
                pe.wait_ge(s_ln, b + 1)
                transposes(xn, b)
            pe.wait_ge(s_mk, 1)
            pe.matmul(ps[0:B * NC, 0, 0:1], cst[0:B * NC, C_BLK:C_BLK + 16], msm[:, 0:1], start=True, stop=True)
            pe.matmul(ps[:, 1, 0:B], msm[:, 0:1].broadcast_to([B * NC, P]), cst[0:B * NC, C_BLK + 16:C_BLK + 16 + B],
                      start=True, stop=True).then_inc(s_mkp, 1)
            pe.wait_ge(s_mk2, 1)
            pe.matmul(ps[0:1, 2, 0:16], msm[:, 3:4], cst[0:B * NC, C_EYE:C_EYE + 16], start=True, stop=True).then_inc(s_lrow, 1)
            pe.wait_ge(s_list, 1)
            NK = B * NF

            def logits(b):
                pe.wait_ge(s_tpf, tp[0])
                o = tp_bank()
                for t in range(TB):
                    for k in range(KC):
                        ins = pe.matmul(o[:, t * E:t * E + E], xnT[:, k, S * b + t * P:S * b + t * P + P], wg[:, k, :],
                                        start=(k == 0), stop=(k == KC - 1))
                ins.then_inc(s_tpr, 1)

            pe.wait_ge(s_wts, 16 * 5)
            for k in range(NK + 2):
                if k < NK:
                    b, f = divmod(k, NF)
                    if f == 0:
                        pe.wait_ge(s_ctxT[b % 2], 16 * (b // 2 + 1))
                        pe.wait_ge(s_tpf, KC * (b + 1) if b < 3 else KC * 4)
                    if k >= 2:
                        pe.wait_ge(s_a, k - 1)
                    for c in range(KC):
                        ins = pe.matmul(ps[:, 4 + k % 2, :], ctxT_s[:, b % 2, c, f * P:f * P + P], xnT[:, c, S * b:S * b + S],
                                        start=(c == 0), stop=(c == KC - 1))
                    ins.then_inc(s_h, 1)
                if k >= 2:
                    b, f = divmod(k - 2, NF)
                    if f == 0:
                        pe.wait_ge(s_ctxN[b % 2], 16 * (b // 2 + 1))
                        if b >= 2:
                            pe.wait_ge(s_res, b - 1)
                    pe.wait_ge(s_a, k - 1)
                    for t in range(TB):
                        ins = pe.matmul(ps[:, b % 2 * 2 + t // 2, t % 2 * D:t % 2 * D + D], hid[:, (k - 2) % 4, t * P:t * P + P], ctxN_s[:, b % 2, f, :],
                                        start=(f == 0 and t % 2 == 0), stop=(f == NF - 1), skip_group_check=True)
                    ins.then_inc(s_mm2, 1)
                if k == 8:
                    pe.wait_ge(s_ln, 3)
                    transposes(xn, 2)
                if k == 20:
                    pe.wait_ge(s_ln, 4)
                    transposes(xn, 3)
                if k == 25:
                    pe.wait_ge(s_ln, 5)
                    transposes(xn, 0)
                    logits(0)
                if k == 38:
                    pe.wait_ge(s_ln, 6)
                    transposes(xn, 1)
                    logits(1)
            for b in range(2, 4):
                pe.wait_ge(s_ln, 5 + b)
                transposes(xn, b)
                logits(b)
            with pe.Fori(0, ROUNDS) as r:
                pe.wait_ge(s_ge, r + 1)
                for t in range(NT):
                    ins = pe.matmul(ps[:, 0, 0:CAND * E], ones_b[:, :], ge_b[:, :, t, :], start=(t == 0), stop=(t == NT - 1))
                ins.then_inc(s_cnt, 1)

            def prefix(dst, src):
                pe.matmul(dst, tri_b[:, :], src, start=True, stop=True, skip_group_check=True)
                for t in range(NT - 1):
                    n = NT - 1 - t
                    ins = pe.matmul(dst[:, (t + 1) * E:], ones_b[:, :], src[:, t, :].unsqueeze(1).broadcast_to([P, n, E]),
                                    start=False, stop=True, skip_group_check=True)
                return ins

            def total(dst, src):
                for t in range(NT):
                    ins = pe.matmul(dst, ones_b[:, :], src[:, t, :], start=(t == 0), stop=(t == NT - 1))
                return ins

            pe.wait_ge(s_gq, 1)
            prefix(ps[:, 1, 0:NT * E], eq_b)
            total(ps[:, 2, 0:E], gt).then_inc(s_gp, 1)
            pe.wait_ge(s_gq, 2)
            prefix(ps[:, 3, 0:NT * E], hot_b)
            total(ps[:, 4, 0:E], hot_b).then_inc(s_gp, 1)

            def block_transposes():
                for j in range(2):
                    for k in range(KC):
                        ins = pe.transpose(ps[:, 6 + j, k * P:k * P + P], xsb[:, j, k * P:k * P + P], eye)
                    ins.then_inc(s_xsTr, 1)

            def experts(i, first_wait, last):
                for j in range(2):
                    e = pe.value_load(be_i[0:1, bass.ds(i * 2 + j, 1)] if not isinstance(i, int) else be_i[0:1, 2 * i + j:2 * i + j + 1],
                                      min_val=0, max_val=E - 1)
                    pe.wait_ge(s_xsT, i * 2 + j + 1)
                    pe.wait_ge(s_ea, i * 2 + j)
                    for k in range(KC):
                        ins = pe.matmul(ps[:, j, :], xsT[:, j, k, :],
                                        w1_s.rearrange("p e k f -> p (e k f)")[:, bass.ds(e * (KC * F) + k * F, F)],
                                        start=(k == 0), stop=(k == KC - 1))
                    ins.then_inc(s_eh, 1)
                for j in range(2):
                    pe.wait_ge(s_ea, i * 2 + j + 1)
                    pe.wait_ge(s_etc, i * 2 + j)
                    for f in range(FC):
                        ins = pe.transpose(ps[:, 2 + j, f * P:f * P + P], hexp[:, j, f * P:f * P + P], eye)
                    ins.then_inc(s_et, 1)
                if not last:
                    pe.wait_ge(s_xsb, (i + 2) * 16)
                    block_transposes()
                for j in range(2):
                    e = pe.value_load(be_i[0:1, bass.ds(i * 2 + j, 1)] if not isinstance(i, int) else be_i[0:1, 2 * i + j:2 * i + j + 1],
                                      min_val=0, max_val=E - 1)
                    pe.wait_ge(s_etc, i * 2 + j + 1)
                    pe.wait_ge(s_eyc, i * 2 + j)
                    for f in range(FC):
                        ins = pe.matmul(ps[:, 4 + j, 0:D], hexpT[:, j, f, :],
                                        w2_s.rearrange("p e f d -> p (e f d)")[:, bass.ds(e * (FC * D) + f * D, D)],
                                        start=(f == 0), stop=(f == FC - 1))
                    ins.then_inc(s_ey, 1)

            pe.wait_ge(s_w12, 16 * 2 * E)
            pe.wait_ge(s_slot, 2)
            pe.wait_ge(s_xsb, 16)
            block_transposes()
            with pe.Fori(0, PAIRS - 1) as i:
                experts(i, None, False)
            experts(PAIRS - 1, None, True)

            pe.wait_ge(s_hot, 16)
            for j in range(NY // 512):
                pe.matmul(ps[0:H, 3 + j, :], relb[:, :], hot_s[0:BUCKETS, j * 512:j * 512 + 512], start=True, stop=True).then_inc(s_dp, 1)
            pe.wait_ge(s_dpc, NY // 512)
            for b in range(B):
                pe.wait_ge(s_ln, 9 + b)
                transposes(xn, b)
                pe.wait_ge(s_tpf, tp[0])
                for m in range(KC):
                    u = KC * b + m
                    if b >= 1:
                        pe.wait_ge(s_qp, b)
                    for k in range(KC):
                        ins = pe.matmul(ps[:, m, :], wq[:, k, m * P:m * P + P], xnT[:, k, S * b:S * b + S],
                                        start=(k == 0), stop=(k == KC - 1))
                    ins.then_inc(s_q, 1)
            pe.wait_ge(s_qp, B)
            n = pe.value_load(lst_i[0:1, 32:33], min_val=1, max_val=B * NC)
            SPB = H * TB // 2
            EPB = CT * H // 2
            with pe.Fori(0, n) as i:
                ci = pe.value_load(lst_i[0:1, bass.ds(i + 16, 1)], min_val=0, max_val=NC - 1)
                pe.wait_ge(s_cc, (i + 1) * 16)
                pe.wait_ge(s_pe, i * EPB)
                for m in range(KC):
                    for k in range(KC):
                        ins = pe.matmul(ps[:, m, :], wk[:, k, m * P:m * P + P], ctx_c[:, k, :], start=(k == 0), stop=(k == KC - 1))
                ins.then_inc(s_kpr, 1)
                for t in range(CT):
                    for k in range(KC):
                        ins = pe.matmul(ps[:, 2 + t // 2, (t % 2) * D:(t % 2) * D + D], ctx_c[:, k, t * P:t * P + P], wv[:, k, :],
                                        start=(k == 0), stop=(k == KC - 1))
                ins.then_inc(s_vpr, 1)
                pe.wait_ge(s_kq, (i + 1) * (16 * 13))
                pe.wait_ge(s_kp, i + 1)
                pe.wait_ge(s_vt, i + 1)
                def scores_for_max(near):
                    for h in range(H):
                        if near and h % HG == 0:
                            pe.wait_ge(s_hk, i * (2 * 16 * NG) + (h // HG + 1) * 16)
                        for jp in range(TB // 2):
                            u = h * (TB // 2) + jp
                            pe.wait_ge(s_scu, i * SPB + (u - 1 if u >= 1 else 0))
                            for j in range(2):
                                ins = pe.matmul(ps[:, 2 * (u % 2) + j, :], Q[0:KR + 1, h, (2 * jp + j) * P:(2 * jp + j + 1) * P],
                                                K[0:KR + 1, h, :], start=True, stop=True, skip_group_check=True)
                                for t in range(CT if near else 0):
                                    x = t * P + (2 * jp + j) * P
                                    ins = pe.matmul(ps[:, 2 * (u % 2) + j, t * P:t * P + P], Hk[:, h % HG, x:x + P], eye,
                                                    start=False, stop=True, skip_group_check=True)
                            ins.then_inc(s_sc, 1)

                with pe.If(ci > 0):
                    scores_for_max(True)
                with pe.Else():
                    scores_for_max(False)
                pe.wait_ge(s_nm, i + 1)
                mt = ps[:, 7, 0:256].bitcast(BF16)
                for j in range(TB):
                    ins = pe.transpose(mt[:, j * P:j * P + P], nmb[:, j, :, :].rearrange("p t h -> p (t h)"), eye_b[:, :])
                ins.then_inc(s_nmt, 1)
                pe.wait_ge(s_mr, (i + 1) * 48)
                def attend(near):
                    for g in range(NG):
                        if near:
                            pe.wait_ge(s_hk, i * (2 * 16 * NG) + (NG + g + 1) * 16)
                        for t in range(CT + 1):
                            for hp in range(HG // 2 if t < CT else 0):
                                u = (g * CT + t) * 2 + hp
                                pe.wait_ge(s_pe, i * EPB + (u - 1 if u >= 1 else 0))
                                for j in range(2):
                                    h = g * HG + hp * 2 + j
                                    ins = pe.matmul(ps[:, 2 * (u % 2) + j, :], K[0:KROWS, h, t * P:t * P + P], Q[0:KROWS, h, :],
                                                    start=True, stop=True, skip_group_check=True)
                                    if near:
                                        ins = pe.matmul(ps[:, 2 * (u % 2) + j, :], eye, Hk[:, hp * 2 + j, t * P:t * P + S],
                                                        start=False, stop=True, skip_group_check=True)
                                ins.then_inc(s_st, 1)
                            if t >= 1:
                                u = (g * CT + t - 1) * 2
                                pe.wait_ge(s_pe, i * EPB + u + 2)
                                if t == 1:
                                    pe.wait_ge(s_oc, i * NG + g)
                                for j in range(HG):
                                    ins = pe.matmul(ps[VW * j:VW * j + VW, 6, :], V[:, t - 1, g * HG + j, :],
                                                    pexp[:, (u + j // 2) % 4, j % 2, :],
                                                    start=(t == 1), stop=(t == CT), tile_position=(0, VW * j))
                                ins.then_inc(s_pv, 1)
                        pe.wait_ge(s_oc, i * NG + g + 1)
                        pe.wait_ge(s_ou, i * NG + g)
                        for j in range(TB):
                            ins = pe.transpose(ps[:, 4, j * P:j * P + P], oT[:, g % 2, j * P:j * P + P], eye)
                        ins.then_inc(s_ot, 1)

                with pe.If(ci > 0):
                    attend(True)
                with pe.Else():
                    attend(False)
            for b in range(B):
                pe.wait_ge(s_acc_f, b + 1)
                transposes(xn, b)
                pe.wait_ge(s_tpf, tp[0])
                if b >= 2:
                    pe.wait_ge(s_res, B + b - 1)
                for t in range(TB):
                    for k in range(KC):
                        ins = pe.matmul(ps[:, b % 2 * 2 + t // 2, t % 2 * D:t % 2 * D + D], xnT[:, k, S * b + t * P:S * b + t * P + P], wo[:, k, :],
                                        start=(k == 0), stop=(k == KC - 1))
                ins.then_inc(s_pj, 1)
            for b in range(B):
                pe.wait_ge(s_ln, 13 + b)
                transposes(xn, b)
            pe.wait_ge(s_tpf, tp[0])
            pe.wait_ge(s_w4, 16 * 6)
            for k in range(KC):
                ins = pe.matmul(ps[:, 0, 0:B], wp1[:, k, :], xnT[:, k, S - 1:T:S], start=(k == 0), stop=(k == KC - 1))
            ins.then_inc(s_nv, 1)
            pe.wait_ge(s_nva, 1)
            pe.matmul(ps[0:B, 1, 0:E], nav[:, :], wp2[:, :], start=True, stop=True).then_inc(s_nl, 1)
            pe.wait_ge(s_sel, 1)
            for b in range(B):
                pe.wait_ge(s_pw[b], 16 * 4)
                for f in range(FC):
                    u = b * FC + f
                    if u >= 2:
                        pe.wait_ge(s_p4a, u - 1)
                    for k in range(KC):
                        ins = pe.matmul(ps[:, u % 2, :], p_w1[:, b, k, f * P:f * P + P], xnT[:, k, S * b:S * b + S],
                                        start=(k == 0), stop=(k == KC - 1))
                    ins.then_inc(s_p4, 1)
                for m in range(KC):
                    u = b * KC + m
                    pe.wait_ge(s_p4a, FC * (b + 1))
                    if b >= 1:
                        pe.wait_ge(s_rtc, u - 1)
                    for f in range(FC):
                        ins = pe.matmul(ps[:, 2 + m, :], p_w2[:, b, f, m * P:m * P + P], hT[:, b % 2, f, :],
                                        start=(f == 0), stop=(f == FC - 1))
                    ins.then_inc(s_rt, 1)
                pe.wait_ge(s_rtc, KC * (b + 1))
                if b >= 1:
                    pe.wait_ge(s_fo, b)
                for t in range(TB):
                    for k in range(KC):
                        ins = pe.matmul(ps[:, 4 + t, 0:D], rT[:, b % 2, k, t * P:t * P + P], wof[:, k, :],
                                        start=(k == 0), stop=(k == KC - 1))
                ins.then_inc(s_po, 1)

        @block.scalar
        def _(act):
            for k in range(B * NF):
                act.wait_ge(s_h, k + 1)
                if k >= 4:
                    act.wait_ge(s_mm2, k - 3)
                act.activation(hid[:, k % 4, :], ps[:, 4 + k % 2, :], ACT.Gelu_apprx_tanh).then_inc(s_a, 1)
            act.wait_ge(s_soft, 1)
            act.activation(t_b[:, :, :], t_a[:, :, :], ACT.Exp).then_inc(s_exp8, 1)
            with act.Fori(0, PAIRS) as i:
                for j in range(2):
                    act.wait_ge(s_eh, i * 2 + j + 1)
                    act.wait_ge(s_et, i * 2 + j)
                    act.activation(hexp[:, j, :], ps[:, j, :], ACT.Gelu).then_inc(s_ea, 1)
                for j in range(2):
                    act.wait_ge(s_ey, i * 2 + j + 1)
                    act.wait_ge(s_ys, i * 16)
                    act.activation(y_s[:, j, :], ps[:, 4 + j, 0:D], ACT.Copy).then_inc(s_eyc, 1)
            act.wait_ge(s_list, 1)
            n = act.value_load(lst_i[0:1, 32:33], min_val=1, max_val=B * NC)
            EPB = CT * H // 2
            with act.Fori(0, n) as i:
                act.wait_ge(s_kpr, i + 1)
                act.wait_ge(s_kst, i * (16 * KC))
                act.activation(kp[:, 0, :, :], ps[:, 0:KC, :], ACT.Copy).then_inc(s_k1, 1)
                act.wait_ge(s_vpr, i + 1)
                act.wait_ge(s_pv, i * (NG * CT))
                act.activation(V[:, :, :, 0:DK], ps[:, 2:4, :].rearrange("p a (t h d) -> p (a t) h d", t=2, d=DK), ACT.Copy).then_inc(s_vt, 1)
                act.wait_ge(s_wgt, i + 1)
                act.activation(scl[:, :, :], dif[:, :, :], ACT.Exp).then_inc(s_wge, 1)
                for u in range(EPB):
                    act.wait_ge(s_st, i * EPB + u + 1)
                    if u >= 4:
                        act.wait_ge(s_pv, i * (NG * CT) + (u - 4) // 2 + 1)
                    act.activation(pexp[:, u % 4, :, :], ps[:, 2 * (u % 2):2 * (u % 2) + 2, :], ACT.Exp).then_inc(s_pe, 1)
            act.wait_ge(s_nv, 1)
            act.activation(nav[:, :], ps[:, 0, 0:B], ACT.Gelu, bias=bp1[:, 0:1]).then_inc(s_nva, 1)
            act.wait_ge(s_l4, 1)
            act.activation(al[0:B, 2, :], al[0:B, 1, :], ACT.Exp).then_inc(s_e4, 1)
            for b in range(B):
                act.wait_ge(s_pw[b], 16 * 4)
                for f in range(FC):
                    act.wait_ge(s_p4, b * FC + f + 1)
                    if b >= 2:
                        act.wait_ge(s_rt, KC * (b - 1))
                    act.activation(hT[:, b % 2, f, :], ps[:, (b * FC + f) % 2, :], ACT.Gelu, bias=p_b1[:, b, f:f + 1]).then_inc(s_p4a, 1)

        @block.vector
        def _(dve):
            ch = Chain(s_dv)
            tp = [0]

            def layer_norm(b):
                for t in range(TB):
                    ins = dve.bn_stats(stats[:, t, :], x_tok[:, TB * b + t, :])
                ch.step(dve, ins)
                for t in range(TB):
                    ins = dve.bn_aggr(mv[:, t, :], stats[:, t, :])
                ch.step(dve, ins)
                ch.step(dve, dve.tensor_scalar(vare[:, :], mv[:, :, 1], EPS, None, ALU.add))
                ch.step(dve, dve.tensor_scalar(rstd[:, :].bitcast(I32), vare[:, :].bitcast(I32), -0.5, float(RSQRT_GUESS), ALU.mult, ALU.add))
                for _ in range(NEWTON):
                    ch.step(dve, dve.tensor_tensor(rsq[:, :], rstd[:, :], rstd[:, :], ALU.mult))
                    ch.step(dve, dve.scalar_tensor_tensor(rsq[:, :], rsq[:, :], -0.5, vare[:, :], ALU.mult, ALU.mult))
                    ch.step(dve, dve.scalar_tensor_tensor(rstd[:, :], rsq[:, :], 1.5, rstd[:, :], ALU.add, ALU.mult))
                for t in range(TB):
                    ins = dve.tensor_scalar(xn[:, TB * b + t, :], x_tok[:, TB * b + t, :], mv[:, t, 0:1], rstd[:, t:t + 1],
                                            ALU.subtract, ALU.mult)
                ins.then_inc(s_ln, 1)

            def take_columns(b):
                for k in range(KC):
                    dve.wait_ge(s_tpr, tp[0] + 1)
                    dve.tensor_copy(xnT[:, k, S * b:S * b + S], ps[:, 6 + tp[0] % 2, :]).then_inc(s_tpf, 1)
                    tp[0] += 1

            def take_logits(b):
                dve.wait_ge(s_tpr, tp[0] + 1)
                dve.tensor_copy(lg[:, TB * b:TB * b + TB, :].rearrange("p t e -> p (t e)"), ps[:, 6 + tp[0] % 2, 0:TB * E]).then_inc(s_tpf, 1)
                tp[0] += 1

            def residual(b, bank):
                for j in range(TB // 2):
                    rows = x_tok[:, TB * b + 2 * j:TB * b + 2 * j + 2, :].rearrange("p t d -> p (t d)")
                    ins = dve.tensor_tensor(rows, rows, ps[:, bank + j, :], ALU.add)
                ins.then_inc(s_res, 1)

            dve.memset(zero_t[:, :], 0.0).then_inc(s_zt, 1)
            dve.wait_ge(s_const, 32)
            dve.tensor_copy(eye_b[:, :], cst[:, C_EYE:C_EYE + P])
            dve.tensor_copy(tri_b[:, :], cst[:, C_TRI:C_TRI + P])
            dve.tensor_copy(ones_b[:, :], cst[:, C_ONES:C_ONES + P]).then_inc(s_bconst, 1)
            for b in range(2):
                dve.wait_ge(s_x[b], 16)
                layer_norm(b)
                take_columns(b)
            dve.wait_ge(s_mask, 48)
            ch.step(dve, dve.tensor_copy(maskw[:, 1, :], mask4[:, :].bitcast(U8)))
            dve.tensor_reduce(msm[:, 0:1], maskw[:, 1, :], AX.X, ALU.max).then_inc(s_mk, 1)
            dve.wait_ge(s_mkp, 1)
            dve.tensor_scalar(a128[:, :], ps[:, 1, 0:B], 1.0, None, ALU.min)
            ch.step(dve, dve.tensor_scalar(msm[:, 1:2], ps[0:B * NC, 0, 0:1], 1.0, None, ALU.min))
            ch.step(dve, dve.tensor_scalar(msm[:, 2:3], msm[:, 1:2], -1.0, 1.0, ALU.mult, ALU.add))
            dve.wait_ge(s_mk, 1)
            dve.tensor_tensor(msm[:, 3:4], msm[:, 2:3], msm[:, 0:1], ALU.max).then_inc(s_mk2, 1)
            ch.step(dve, dve.scalar_tensor_tensor(maskw[:, 2, :], maskw[:, 0, :], msm[:, 2:3], maskw[:, 1, :], ALU.mult, ALU.max))
            dve.tensor_scalar(mrow_b[:, :], maskw[:, 2, :], 1.0, -NEG, ALU.subtract, ALU.mult).then_inc(s_mrow, 1)
            dve.wait_ge(s_lrow, 1)
            ch.step(dve, dve.tensor_copy(lst[:, 0, :], ps[0:1, 2, 0:16]))
            ch.step(dve, dve.tensor_tensor_scan(lst[:, 1, :], cst[0:1, C_ONES:C_ONES + 16], lst[:, 0, :], 0.0, ALU.mult, ALU.add))
            ch.step(dve, dve.tensor_tensor(lst2[:, :, :], lst[:, 1, :].unsqueeze(1).broadcast_to([1, 16, 16]),
                                           cst[0:1, C_LIST + 32:C_LIST + 48].unsqueeze(2).broadcast_to([1, 16, 16]), ALU.is_equal))
            ch.step(dve, dve.tensor_tensor(lst2[:, :, :], lst2[:, :, :], lst[:, 0, :].unsqueeze(1).broadcast_to([1, 16, 16]), ALU.mult))
            for q in range(2):
                ch.step(dve, dve.tensor_tensor(lst3[:, :, :], lst2[:, :, :],
                                               cst[0:1, C_LIST + 16 * q:C_LIST + 16 * q + 16].unsqueeze(1).broadcast_to([1, 16, 16]), ALU.mult))
                ch.step(dve, dve.tensor_reduce(lst[:, 2 + q, :], lst3[:, :, :], AX.X, ALU.add))
                dve.tensor_copy(lst_i[:, 16 * q:16 * q + 16], lst[:, 2 + q, :])
            dve.tensor_copy(lst_i[:, 32:33], lst[:, 1, 15:16]).then_inc(s_list, 1)
            for b in range(2, 4):
                dve.wait_ge(s_x[b], 16)
                layer_norm(b)
                if b == 2:
                    take_columns(b)
            for b in range(B):
                dve.wait_ge(s_mm2, NF * (b + 1))
                residual(b, b % 2 * 2)
                dve.wait_ge(s_res, b + 1)
                if b == 0:
                    take_columns(3)
                layer_norm(b)
                if b < 2:
                    take_columns(b)
                    take_logits(b)
            for b in range(2, 4):
                take_columns(b)
                take_logits(b)
            dve.wait_ge(s_tpf, tp[0])
            ch.step(dve, dve.tensor_reduce(r16[:, :], lg[:, :, :], AX.X, ALU.max))

            def wide(v):
                return v.unsqueeze(2).broadcast_to([P, NT, E])

            def by_expert(v):
                return v.unsqueeze(1).broadcast_to([P, NT, E])

            dve.tensor_tensor(t_a[:, :, :], lg[:, :, :], wide(r16), ALU.subtract).then_inc(s_soft, 1)
            dve.memset(ones8[:, :], 1.0)
            dve.memset(cur[:, :], 0)
            dve.wait_ge(s_exp8, 1)
            ch.step(dve, dve.tensor_reduce(r16[:, :], t_b[:, :, :], AX.X, ALU.add))
            ch.step(dve, dve.reciprocal(gate[:, :], r16[:, :]))
            ch.step(dve, dve.tensor_tensor(pr[:, :, :], t_b[:, :, :], wide(gate), ALU.mult))
            STEPS = 5
            base = ch.n
            with dve.Fori(0, ROUNDS) as r:
                c3 = Chain(s_dvr, r * STEPS)
                c3.step(dve, dve.tensor_tensor(cand[:, :, :], cur.unsqueeze(1).broadcast_to([P, CAND, E]),
                                               cand_c[:, bass.ds(r * CAND, CAND)].unsqueeze(2).broadcast_to([P, CAND, E]), ALU.bitwise_or))
                for c in range(CAND):
                    ins = dve.tensor_tensor(ge_b[:, c, :, :], pr[:, :, :],
                                            cand[:, c, :].bitcast(F32).unsqueeze(1).broadcast_to([P, NT, E]), ALU.is_ge)
                ins.then_inc(s_ge, 1)
                dve.wait_ge(s_cnt, r + 1)
                c3.step(dve, dve.tensor_scalar(npass.rearrange("p c e -> p (c e)"), ps[:, 0, 0:CAND * E], CAP - 0.5, None, ALU.is_gt))
                c3.step(dve, dve.tensor_reduce(nsum[:, :], npass.rearrange("p c e -> p e c"), AX.X, ALU.add))
                c3.step(dve, dve.tensor_scalar(ninc[:, :], nsum[:, :], cst[:, bass.ds(r + C_STEP, 1)], None, ALU.mult))
                c3.step(dve, dve.tensor_tensor(cur[:, :], cur[:, :], ninc[:, :], ALU.bitwise_or))
            thr = cur.bitcast(F32)
            dve.tensor_tensor(gt[:, :, :], pr[:, :, :], by_expert(thr), ALU.is_gt)
            dve.tensor_tensor(eq_b[:, :, :], pr[:, :, :], by_expert(thr), ALU.is_equal).then_inc(s_gq, 1)
            dve.wait_ge(s_gp, 1)
            ch.step(dve, dve.tensor_scalar(need[:, :], ps[:, 2, 0:E], -1.0, float(CAP), ALU.mult, ALU.add))
            ch.step(dve, dve.tensor_tensor(t_a[:, :, :], ps[:, 1, 0:NT * E].rearrange("p (t e) -> p t e", e=E), by_expert(need), ALU.is_lt))
            ch.step(dve, dve.tensor_tensor(t_a[:, :, :], t_a[:, :, :], eq_b[:, :, :], ALU.mult))
            ch.step(dve, dve.tensor_tensor(sel[:, :, :], t_a[:, :, :], gt[:, :, :], ALU.add))
            ch.step(dve, dve.tensor_reduce(asg[:, :], sel[:, :, :], AX.X, ALU.max))
            ch.step(dve, dve.tensor_tensor(t_a[:, :, :], wide(asg), sel[:, :, :], ALU.subtract))
            ch.step(dve, dve.scalar_tensor_tensor(t_b[:, :, :], t_a[:, :, :], -2.0, pr[:, :, :], ALU.mult, ALU.add))
            ch.step(dve, dve.tensor_reduce(gate[:, :], t_b[:, :, :], AX.X, ALU.max))
            ch.step(dve, dve.tensor_tensor(t_a[:, :, :], t_b[:, :, :], wide(gate), ALU.is_equal))
            ch.step(dve, dve.tensor_tensor(t_a[:, :, :], t_a[:, :, :], by_expert(cst[:, C_EM8:C_EM8 + E]), ALU.mult))
            ch.step(dve, dve.tensor_reduce(r16[:, :], t_a[:, :, :], AX.X, ALU.min))
            dve.tensor_tensor(hot_b[:, :, :], by_expert(cst[:, C_EM8:C_EM8 + E]), wide(r16), ALU.is_equal).then_inc(s_gq, 1)
            dve.wait_ge(s_gp, 2)
            ch.step(dve, dve.tensor_tensor(nbw[:, :, :], ps[:, 4, 0:E].unsqueeze(2).broadcast_to([P, E, NT]),
                                           cst[:, C_JT:C_JT + NT].unsqueeze(1).broadcast_to([P, E, NT]), ALU.is_gt))
            ch.step(dve, dve.tensor_reduce(nb[:, :], nbw[:, :, :], AX.X, ALU.add))
            ch.step(dve, dve.tensor_tensor_scan(cb[:, :], ones8[:, :], nb[:, :], 0.0, ALU.mult, ALU.add))
            ch.step(dve, dve.tensor_tensor(base_s[:, :], cb[:, :], nb[:, :], ALU.subtract))
            ch.step(dve, dve.scalar_tensor_tensor(t_a[:, :, :], by_expert(base_s), float(P), ps[:, 3, 0:NT * E].rearrange("p (t e) -> p t e", e=E),
                                                  ALU.mult, ALU.add))
            dve.wait_ge(s_gq, 2)
            ch.step(dve, dve.tensor_tensor(t_a[:, :, :], t_a[:, :, :], hot_b[:, :, :], ALU.mult))
            ch.step(dve, dve.tensor_reduce(r16[:, :], t_a[:, :, :], AX.X, ALU.add))
            dve.tensor_copy(slot_i[:, :], r16[:, :]).then_inc(s_slot, 1)
            ch.step(dve, dve.tensor_tensor(be_w[:, :, :], cb.unsqueeze(1).broadcast_to([P, NBLK, E]),
                                           cst[:, C_JB:C_JB + NBLK].unsqueeze(2).broadcast_to([P, NBLK, E]), ALU.is_le))
            ch.step(dve, dve.tensor_reduce(be[:, :], be_w[:, :, :], AX.X, ALU.add))
            dve.tensor_scalar(be_i[:, :], be[:, :], float(E - 1), None, ALU.min).then_inc(s_slot, 1)
            for j in range(2):
                dve.wait_ge(s_xsTr, j + 1)
                dve.tensor_copy(xsT[:, j, :, :].rearrange("p k n -> p (k n)"), ps[:, 6 + j, 0:KC * P]).then_inc(s_xsT, 1)
            with dve.Fori(0, PAIRS - 1) as i:
                for j in range(2):
                    dve.wait_ge(s_et, i * 2 + j + 1)
                    dve.wait_ge(s_ey, i * 2 + j)
                    dve.tensor_copy(hexpT[:, j, :, :].rearrange("p k n -> p (k n)"), ps[:, 2 + j, :]).then_inc(s_etc, 1)
                for j in range(2):
                    dve.wait_ge(s_xsTr, i * 2 + j + 3)
                    dve.tensor_copy(xsT[:, j, :, :].rearrange("p k n -> p (k n)"), ps[:, 6 + j, 0:KC * P]).then_inc(s_xsT, 1)
            for j in range(2):
                u = 2 * (PAIRS - 1) + j
                dve.wait_ge(s_et, u + 1)
                dve.wait_ge(s_ey, u)
                dve.tensor_copy(hexpT[:, j, :, :].rearrange("p k n -> p (k n)"), ps[:, 2 + j, :]).then_inc(s_etc, 1)
            dve.wait_ge(s_gat, 16 * NT)
            for t in range(NT):
                ins = dve.scalar_tensor_tensor(x_tok[:, t, :], yg[:, t, :], gate[:, t:t + 1], x_tok[:, t, :], ALU.mult, ALU.add)
            ch.step(dve, ins)
            dve.memset(V[:, :, :, :], 0.0)
            dve.memset(acc[:, :, :, :, :], 0.0)
            dve.memset(nmb[:, :, :, :], 0.0)
            dve.memset(m_run[:, :, :], NEG).then_inc(s_init3, 1)
            for j in range(NY // 512):
                dve.wait_ge(s_dp, j + 1)
                dve.tensor_copy(dist_s[0:H, j * 512:j * 512 + 512], ps[0:H, 3 + j, :]).then_inc(s_dpc, 1)
            dve.wait_ge(s_dpc, NY // 512)
            for b in range(B):
                if b >= 1:
                    dve.wait_ge(s_dstore, 16 * b)
                dve.tensor_scalar(dist_g[0:H, :], dist_s[0:H, :], a128[0:H, b:b + 1], None, ALU.mult).then_inc(s_dst, 1)
            for b in range(B):
                layer_norm(b)
            for b in range(B):
                take_columns(b)
                for m in range(KC):
                    dve.wait_ge(s_q, KC * b + m + 1)
                    if b >= 1:
                        dve.wait_ge(s_qst, 16 * KC * b)
                    ch.step(dve, dve.tensor_scalar(qf[:, :], ps[:, m, :], a128[:, b:b + 1], None, ALU.mult))
                    ch.step(dve, dve.tensor_copy(qp[:, 0, m, :], qf[:, :]))
                    ch.step(dve, dve.tensor_tensor(qr[:, :], qf[:, :], qp[:, 0, m, :], ALU.subtract))
                    ch.step(dve, dve.tensor_copy(qp[:, 1, m, :], qr[:, :]))
                    ins = dve.tensor_tensor(qp[:, 2, m, :], qr[:, :], qp[:, 1, m, :], ALU.subtract)
                ins.then_inc(s_qp, 1)
            dve.wait_ge(s_dstore, 16 * B)
            dve.memset(Q[KR:KROWS, :, :], 1.0)
            dve.memset(K[KR:KROWS, :, :], 1.0)
            dve.memset(V[:, :, :, DK:DK + 1], 1.0).then_inc(s_rows, 1)
            n = dve.value_load(lst_i[0:1, 32:33], min_val=1, max_val=B * NC)
            SPB = H * TB // 2
            STEPS3 = 9
            with dve.Fori(0, n) as i:
                c3 = Chain(s_dv3, i * STEPS3)
                bi = dve.value_load(lst_i[0:1, bass.ds(i, 1)], min_val=0, max_val=B - 1)
                dve.wait_ge(s_k1, i + 1)
                c3.step(dve, dve.tensor_tensor(kf[:, :, :], ps[:, 0:KC, :], kp[:, 0, :, :], ALU.subtract))
                c3.step(dve, dve.tensor_copy(kp[:, 1, :, :], kf[:, :, :]))
                dve.tensor_tensor(kp[:, 2, :, :], kf[:, :, :], kp[:, 1, :, :], ALU.subtract).then_inc(s_kp, 1)
                for u in range(SPB):
                    h, jp = divmod(u, TB // 2)
                    dve.wait_ge(s_sc, i * SPB + u + 1)
                    dve.tensor_reduce(cmax[:, h, 2 * jp:2 * jp + 2], ps[:, 2 * (u % 2):2 * (u % 2) + 2, :], AX.X, ALU.max).then_inc(s_scu, 1)
                dve.wait_ge(s_scu, (i + 1) * SPB)
                c3.step(dve, dve.tensor_scalar(nm[:, :, :], cmax[:, :, :], -1.0, None, ALU.mult))
                nmv = nm.rearrange("p h j -> p j h")
                rv = nmr.rearrange("p h j -> p j h")
                c3.step(dve, dve.tensor_copy(nmb[:, :, 0, :], nmv))
                c3.step(dve, dve.tensor_tensor(rv, nmv, nmb[:, :, 0, :], ALU.subtract))
                c3.step(dve, dve.tensor_copy(nmb[:, :, 1, :], rv))
                dve.tensor_tensor(nmb[:, :, 2, :], rv, nmb[:, :, 1, :], ALU.subtract).then_inc(s_nm, 1)
                cm = cmax.rearrange("p h j -> p (h j)")
                run = m_run[:, bass.ds(bi, 1), :].rearrange("p b c -> p (b c)")
                c3.step(dve, dve.tensor_tensor(m_new[:, :], run, cm, ALU.max))
                dve.wait_ge(s_wge, i)
                dve.tensor_tensor(dif[:, 0, :], run, m_new[:, :], ALU.subtract)
                c3.step(dve, dve.tensor_tensor(dif[:, 1, :], cm, m_new[:, :], ALU.subtract))
                c3.step(dve, dve.tensor_tensor(run, m_new[:, :], m_new[:, :], ALU.max))
                dve.tensor_copy(m_new[:, 0:1], m_new[:, 0:1]).then_inc(s_wgt, 1)
                dve.wait_ge(s_nmt, i + 1)
                dve.wait_ge(s_mr, i * 48)
                dve.tensor_copy(mrow[0:3 * H, :], ps[0:3 * H, 7, 0:256].bitcast(BF16)).then_inc(s_nmc, 1)
                for g in range(NG):
                    dve.wait_ge(s_pv, i * (NG * CT) + (g + 1) * CT)
                    dve.tensor_copy(oT[:, g % 2, :], ps[:, 6, :]).then_inc(s_oc, 1)
                    if g == 0:
                        dve.wait_ge(s_wge, i + 1)

                    def weight(w):
                        return (scl[:, w, g * HG * TB:(g + 1) * HG * TB].rearrange("p (h j) -> p j h", j=TB)
                                .unsqueeze(3).broadcast_to([P, TB, HG, DK + 1]))

                    av = acc[:, bass.ds(bi, 1), :, g * HG:(g + 1) * HG, :].rearrange("p b j h d -> p (b j) h d")
                    dve.tensor_tensor(av, av, weight(0), ALU.mult)
                    dve.wait_ge(s_ot, i * NG + g + 1)
                    dve.tensor_tensor(tmp[:, :, :, :], ps[:, 4, :].rearrange("p (j h v) -> p j h v", j=TB, h=HG)[:, :, :, 0:DK + 1],
                                      weight(1), ALU.mult).then_inc(s_dvm, 1)
                    dve.wait_ge(s_dvm, i * NG + g + 1)
                    dve.tensor_tensor(av, av, tmp[:, :, :, :], ALU.add).then_inc(s_ou, 1)
            dve.wait_ge(s_ou, n * NG)
            accv = acc.rearrange("p b j h d -> p (b j) h d")
            ch.step(dve, dve.reciprocal(rl.unsqueeze(3), accv[:, :, :, DK:DK + 1]))
            for b in range(B):
                dve.tensor_tensor(xn[:, TB * b:TB * b + TB, :].rearrange("p t (h d) -> p t h d", d=DK),
                                  accv[:, TB * b:TB * b + TB, :, 0:DK],
                                  rl[:, TB * b:TB * b + TB, :].unsqueeze(3).broadcast_to([P, TB, H, DK]), ALU.mult).then_inc(s_acc_f, 1)
            for b in range(B):
                take_columns(b)
                dve.wait_ge(s_pj, b + 1)
                residual(b, b % 2 * 2)
            dve.wait_ge(s_res, 2 * B)
            for b in range(B):
                layer_norm(b)
            for b in range(B):
                take_columns(b)
            dve.wait_ge(s_nl, 1)
            dve.wait_ge(s_w4, 16 * 6)
            ch.step(dve, dve.tensor_tensor(al[0:B, 0, :], ps[0:B, 1, 0:E], bp2[0:B, :], ALU.add))
            ch.step(dve, dve.tensor_reduce(al[0:B, 7, 0:1], al[0:B, 0, :], AX.X, ALU.max))
            dve.tensor_scalar(al[0:B, 1, :], al[0:B, 0, :], al[0:B, 7, 0:1], None, ALU.subtract).then_inc(s_l4, 1)
            dve.wait_ge(s_e4, 1)
            ch.step(dve, dve.tensor_reduce(al[0:B, 7, 1:2], al[0:B, 2, :], AX.X, ALU.add))
            ch.step(dve, dve.reciprocal(al[0:B, 7, 4:5], al[0:B, 7, 1:2]))
            ch.step(dve, dve.tensor_scalar(al[0:B, 3, :], al[0:B, 2, :], al[0:B, 7, 4:5], None, ALU.mult))
            ch.step(dve, dve.tensor_reduce(al[0:B, 7, 2:3], al[0:B, 3, :], AX.X, ALU.max))
            ch.step(dve, dve.tensor_scalar(al[0:B, 4, :], al[0:B, 3, :], al[0:B, 7, 2:3], None, ALU.is_equal))
            ch.step(dve, dve.tensor_tensor(al[0:B, 5, :], al[0:B, 4, :], cst[0:B, C_EM8:C_EM8 + E], ALU.mult))
            ch.step(dve, dve.tensor_reduce(al[0:B, 7, 3:4], al[0:B, 5, :], AX.X, ALU.min))
            dve.tensor_scalar(sel_i[0:B, 0:1], al[0:B, 7, 3:4], float(E), None, ALU.add).then_inc(s_sel, 1)
            ch.step(dve, dve.tensor_scalar(bo_s[:, :], bo_s[:, :], 0.3, None, ALU.mult))
            dve.tensor_tensor(base4[:, :, :], xn[:, :, :], bo_s.unsqueeze(1).broadcast_to([P, NT, D]), ALU.add).then_inc(s_base, 1)
            dve.wait_ge(s_base, 1)
            ch.step(dve, dve.tensor_tensor(base4[:, :, :], base4[:, :, :], x_tok[:, :, :], ALU.add))
            for b in range(B):
                for m in range(KC):
                    dve.wait_ge(s_rt, KC * b + m + 1)
                    dve.tensor_scalar(rT[:, b % 2, m, :], ps[:, 2 + m, :], p_b2[:, b, m:m + 1], None, ALU.add).then_inc(s_rtc, 1)
                dve.wait_ge(s_po, b + 1)
                for t in range(TB):
                    ins = dve.scalar_tensor_tensor(o_s[:, TB * b + t, :], ps[:, 4 + t, 0:D], 0.3, base4[:, TB * b + t, :], ALU.mult, ALU.add)
                ins.then_inc(s_fo, 1)

        @block.gpsimd
        def _(pool):
            pool.wait_ge(s_slot, 1)
            pool.wait_ge(s_ln, 2 * B)
            pool.wait_ge(s_zero, 16)
            for t in range(NT):
                pool.indirect_dma_start(xs_d, bass.IndirectOffsetOnAxis(ap=slot_i[:, t:t + 1].bitcast(U32), axis=0),
                                        xn[:, t, :], None).then_inc(s_scat, 16)
            pool.wait_ge(s_ys, 16 * PAIRS)
            for t in range(NT):
                pool.indirect_dma_start(yg[:, t, :], None, ys_d,
                                        bass.IndirectOffsetOnAxis(ap=slot_i[:, t:t + 1].bitcast(U32), axis=0)).then_inc(s_gat, 16)


NAMES = {
    "x": [T, D], "ctxT": [B, D, LP], "ctxN": [B, NF * P, D], "mask": [B * NC, CH // 4], "Wg": [D, E], "W1": [E, D, F], "W2": [E, F, D],
    "WqT": [D, D], "WkT": [D, D], "WvT": [D, D], "WoT": [D, D], "rel_biasT": [BUCKETS, H], "Wp1": [D, NAV], "bp1": [NAV],
    "Wp2": [NAV, E], "bp2": [E], "pW1": [E, D, F], "pb1": [E, F], "pW2": [E, F, D], "pb2": [E, D], "Wof": [D, D], "bo": [D],
}


def lay_out(x, ctx_1024, mask_Bx1x1xS2_bk0, L0_ffn_Wg, L0_ffn_W1, L0_ffn_W2, L1_xattn_Wq, L1_xattn_Wk, L1_xattn_Wv, L1_xattn_Wo,
            L1_xattn_rel_bias, L1_ffn_Wp1, L1_ffn_bp1, L1_ffn_Wp2, L1_ffn_bp2, L1_ffn_W1, L1_ffn_b1, L1_ffn_W2, L1_ffn_b2, L1_ffn_Wo, L1_ffn_bo):
    c = np.asarray(ctx_1024)[:, ::-1, :]
    ctxT = np.zeros((B, D, LP), np.float32)
    ctxT[:, :, 0:L] = c.transpose(0, 2, 1)
    ctxN = np.zeros((B, NF * P, D), np.float32)
    ctxN[:, 0:L, :] = c
    mask = np.zeros((B, LP), np.uint8)
    mask[:, 0:L] = np.asarray(mask_Bx1x1xS2_bk0).reshape(B, L)[:, ::-1].view(np.uint8)
    arrays = {
        "x": np.asarray(x).reshape(T, D), "ctxT": ctxT, "ctxN": ctxN, "mask": mask.reshape(B * NC, CH).view(np.int32),
        "Wg": L0_ffn_Wg, "W1": L0_ffn_W1, "W2": L0_ffn_W2,
        "WqT": np.asarray(L1_xattn_Wq).T, "WkT": np.asarray(L1_xattn_Wk).T, "WvT": np.asarray(L1_xattn_Wv).T,
        "WoT": np.asarray(L1_xattn_Wo).T, "rel_biasT": np.asarray(L1_xattn_rel_bias).T,
        "Wp1": L1_ffn_Wp1, "bp1": L1_ffn_bp1, "Wp2": L1_ffn_Wp2, "bp2": L1_ffn_bp2, "pW1": L1_ffn_W1, "pb1": L1_ffn_b1,
        "pW2": L1_ffn_W2, "pb2": L1_ffn_b2, "Wof": L1_ffn_Wo, "bo": L1_ffn_bo,
    }
    arrays = {k: np.ascontiguousarray(np.asarray(v)) for k, v in arrays.items()}
    arrays.update(shape_constants())
    return arrays


def program(nc):
    shapes = {k: (v, I32 if k == "mask" else F32) for k, v in NAMES.items()}
    for k, v in shape_constants().items():
        shapes[k] = (list(v.shape), mybir.dt.from_np(v.dtype))
    a = {k: nc.dram_tensor(f"in_{k}", s, dt, kind="ExternalInput").ap() for k, (s, dt) in shapes.items()}
    a["out"] = nc.dram_tensor("out_0", [T, D], F32, kind="ExternalOutput").ap()
    build(nc, a)


def kernel(**inputs):
    import concourse.bacc as bacc
    from concourse.bass_utils import run_bass_kernel_spmd
    nc = bacc.Bacc("TRN2", target_bir_lowering=False, num_devices=1)
    program(nc)
    arrays = {f"in_{k}": v for k, v in lay_out(**inputs).items()}
    r = run_bass_kernel_spmd(nc, [arrays], core_ids=[0])
    return r.results[0]["out_0"].reshape(B, S, D)
```

```python
from contextlib import ExitStack
import math

import numpy as np
import concourse.bass as bass
from concourse import mybir
from concourse.alu_op_type import AluOpType as ALU

ACT = mybir.ActivationFunctionType
AX = mybir.AxisListType
F32 = mybir.dt.float32
BF16 = mybir.dt.bfloat16
I32 = mybir.dt.int32
U32 = mybir.dt.uint32
U8 = mybir.dt.uint8

P = 128
B, S, D = 4, 512, 256
L = 1601
T = B * S
NT = T // P
TB = S // P
KC = D // P
NF = -(-L // P)
E, F = 8, 512
FC = F // P
CAP = T // E
NBLK = 24
PAIRS = NBLK // 2
H, DK = 16, 16
CH = 512
NC = -(-L // CH)
LP = NC * CH
CT = CH // P
HG = 4
NG = H // HG
HH = H // 2
AU = H * TB
A_T0 = AU // 2 + 6
A_T1 = AU + 1
APB = AU + 2
TURN, PROJECT, TURN4 = {1: 0, 4: 1, 8: 2}, {2: 0, 5: 1, 9: 2}, {4: 0, 8: 1, 12: 2}
TURNS_BEFORE = 2 * KC * B + B
ROUTE = 13
VW = 32
TERMS = 6
KR = TERMS * DK
ROW_MASK = KR
ROW_MAX = KR + 1
KROWS = KR + 4
BUCKETS, MAX_DISTANCE = 32, 128
NY = LP + S
HW_ = S + CH - P
NEG = -1.0e30
EPS = 1e-5
RSQRT_GUESS, NEWTON = 0x5F3759DF, 3
NAV = 128
SEARCH_BITS = 3
ROUNDS = 30 // SEARCH_BITS
CAND = 2 ** SEARCH_BITS - 1


def shape_constants():
    eye = np.eye(P, dtype=np.float32)
    tri = np.triu(np.ones((P, P), np.float32), 1)
    ones = np.ones((P, P), np.float32)
    em8 = np.tile(np.arange(E, dtype=np.float32) - E, (P, 1))
    jt = np.tile(np.arange(NT, dtype=np.float32) * P, (P, 1))
    jb = np.tile(np.arange(NBLK, dtype=np.float32), (P, 1))
    steps = np.zeros((P, ROUNDS), np.float32)
    for r in range(ROUNDS):
        steps[:, r] = 2.0 ** (30 - SEARCH_BITS * (r + 1))
    blk = np.zeros((P, 64), np.float32)
    for i in range(B * NC):
        blk[i, (i // NC) * NC:(i // NC + 1) * NC] = 1.0
        blk[i, 16 + i // NC] = 1.0
        blk[i, 32] = i // NC
        blk[i, 33] = i % NC
    lists = np.zeros((P, 48), np.float32)
    lists[:, 0:16] = np.arange(16) // NC
    lists[:, 16:32] = np.arange(16) % NC
    lists[:, 32:48] = np.arange(16) + 1
    f32 = np.concatenate([eye, tri, ones, em8, jt, jb, steps, blk, lists], axis=1)
    cand = np.zeros((P, ROUNDS * CAND), np.int32)
    for r in range(ROUNDS):
        for c in range(CAND):
            cand[:, r * CAND + c] = (c + 1) << (30 - SEARCH_BITS * (r + 1))
    real = np.zeros((B * NC, CH), np.float32)
    for i in range(B * NC):
        real[i] = (np.arange(CH) + CH * (i % NC)) < L
    rel = (L - 1) - np.arange(NY)
    rp = np.abs(rel)
    half, exact = BUCKETS // 2, BUCKETS // 4
    large = exact + (np.log(np.maximum(rp, 1).astype(np.float32) / np.float32(exact))
                     / np.float32(math.log(MAX_DISTANCE / exact)) * np.float32(half - exact)).astype(np.int32)
    bucket = np.where(rel > 0, half, 0) + np.where(rp < exact, rp, np.minimum(large, half - 1))
    hot = np.zeros((BUCKETS, NY), np.float32)
    hot[bucket, np.arange(NY)] += 1.0
    hot[BUCKETS - 1] -= 1.0
    return {"c_f32": f32, "c_cand": cand, "c_real": real, "c_hot": hot}


C_EYE, C_TRI, C_ONES, C_EM8 = 0, P, 2 * P, 3 * P
C_JT = C_EM8 + E
C_JB = C_JT + NT
C_STEP = C_JB + NBLK
C_BLK = C_STEP + ROUNDS
C_LIST = C_BLK + 64
C_END = C_LIST + 48


class Chain:

    def __init__(self, sem, base=0):
        self.sem, self.n, self.base = sem, 0, base

    def add(self, ins):
        self.n += 1
        ins.then_inc(self.sem, 1)

    def settle(self, eng):
        eng.wait_ge(self.sem, self.base + self.n)

    def step(self, eng, ins):
        self.add(ins)
        self.settle(eng)


def build(nc, a):
    with ExitStack() as ctx:
        def sb(name, shape, dt):
            return ctx.enter_context(nc.sbuf_tensor(name, shape, dt))

        def sem(name):
            return ctx.enter_context(nc.semaphore(name))

        def dram(name, shape, dt):
            return nc.dram_tensor(name, shape, dt, kind="Internal").ap()

        xs_d = dram("xs_sorted", [(NBLK + 2) * P, D], F32)
        ys_d = dram("ys_sorted", [NBLK * P, D], F32)
        q_d = dram("q_parts", [B, 3, DK, H, S], BF16)
        k_d = dram("k_parts", [3, D, CH], BF16)
        k0_d = dram("last_k_parts", [B, 3, DK, H, CH], BF16)
        v0_d = dram("last_v", [B, P, CT * H * VW], F32)
        mask_d = dram("mask_rows", [B * NC, CH], BF16)
        dist_d = dram("bias_by_distance", [B, H, NY], F32)

        x_tok = sb("x_tok", [P, NT, D], F32)
        xn = sb("xn", [P, NT, D], F32)
        xnT = sb("xnT", [P, KC, T], F32)
        cst = sb("cst", [P, C_END], F32)
        cand_c = sb("cand_c", [P, ROUNDS * CAND], I32)
        eye_b = sb("eye_b", [P, P], BF16)
        tri_b = sb("tri_b", [P, P], BF16)
        ones_b = sb("ones_b", [P, P], BF16)
        eye = cst[:, C_EYE:C_EYE + P]
        wq = sb("wq", [P, KC, D], F32)
        wk = sb("wk", [P, KC, D], F32)
        wv = sb("wv", [P, KC, D], F32)
        wo = sb("wo", [P, KC, D], F32)
        wg = sb("wg", [P, KC, E], F32)
        relb = sb("relb", [BUCKETS, H], F32)
        lg = sb("router_logits", [P, NT, E], F32)
        zero_t = sb("zero_tile_s", [P, D], F32)
        stats = sb("stats", [P, NT, 6], F32)
        mv = sb("mv", [P, NT, 2], F32)
        rstd = sb("rstd", [P, NT], F32)
        nmr_ = sb("minus_mean_by_root", [P, NT], F32)
        vare = sb("var_eps", [P, NT], F32)
        rsq = sb("root_squared", [P, NT], F32)
        a128 = sb("a128", [P, B], F32)
        maskw = sb("maskw", [B * NC, 4, CH], F32)
        mask4 = sb("mask4", [B * NC, CH // 4], I32)
        mrow_b = sb("mrow_b", [B * NC, CH], BF16)
        msm = sb("msm", [B * NC, 8], F32)
        lst = sb("lst", [1, 8, 16], F32)
        lst2 = sb("lst2", [1, 16, 16], F32)
        lst3 = sb("lst3", [1, 16, 16], F32)
        lst_i = sb("lst_i", [1, 40], I32)

        A_MAX = 33024
        arena = sb("arena", [P, A_MAX], F32)
        at = [0]

        def view(shape, dt=F32, off=None):
            n = int(np.prod(shape))
            words = n if dt in (F32, I32, U32) else -(-n // 2)
            o = at[0] if off is None else off
            at[0] = o + words
            assert at[0] <= A_MAX, at[0]
            v = arena[:, o:o + words]
            if dt != F32:
                v = v.bitcast(dt)[:, 0:n]
            if len(shape) > 1:
                names = "abcd"[:len(shape)]
                v = v.rearrange(f"p ({' '.join(names)}) -> p {' '.join(names)}",
                                **{k: s for k, s in zip(names[1:], shape[1:])})
            return v

        ctxT_s = view([2, KC, NF * P])
        ctxN_s = view([2, NF, D])
        hid = view([4, S])
        part1_end = at[0]
        w1_s = view([E, KC, F])
        w2_s = view([E, FC, D])
        at[0] = 0
        pr = view([NT, E]); sel = view([NT, E]); gt = view([NT, E], BF16)
        t_a = view([NT, E]); t_b = view([NT, E])
        hot_b = view([NT, E], BF16); eq_b = view([NT, E], BF16)
        ge_b = view([CAND, NT, E], BF16)
        cand = view([CAND, E], I32); cur = view([E], I32); npass = view([CAND, E]); nsum = view([E]); ninc = view([E], I32)
        r16 = view([NT]); gate = view([NT]); asg = view([NT])
        need = view([E]); nb = view([E]); cb = view([E]); base_s = view([E]); ones8 = view([E]); nbw = view([E, NT])
        slot_i = view([NT], I32)
        be = view([NBLK]); be_w = view([NBLK, E]); be_i = view([NBLK + 2], I32); pw = view([PAIRS])
        xsb = view([2, D]); xsT = view([2, KC, P]); hexp = view([2, F]); hexpT = view([2, FC, P])
        y_s = view([2, D])
        yg_at = at[0]
        yg = view([NT, D])
        ctx_e = view([2, KC, CH])
        kp_e = view([3, KC, CH], BF16); kr_e = view([2, CH])
        part2_end = at[0]
        v_e = [view([2, CT, H, VW], off=yg_at), view([2, CT, H, VW], off=part1_end)]
        at[0] = part2_end
        assert at[0] <= part1_end, (at[0], part1_end)
        at[0] = 0
        ctx_c = view([KC, CH])
        kp = view([3, KC, CH], BF16); kf = view([KC, CH])
        q_at = at[0]
        Q = view([H, S], BF16); K = view([H, CH], BF16)
        v_at = at[0]
        V = view([CT, H, VW])
        pexp = view([4, 2, S])
        mrow = view([S], BF16)
        cmax = view([H, TB]); nm = view([H, TB]); nmr = view([H, TB])
        nmb = view([TB, P // H, H], BF16)
        m_run = view([B, H * TB]); m_new = view([H * TB]); dif = view([2, H * TB]); scl = view([2, H * TB])
        acc = view([B, TB, H, DK + 1]); tmp = view([TB, HG, DK + 1]); oT = view([2, S])
        Hk = view([HG, HW_])
        rl = view([NT, H])
        part3_end = at[0]
        at[0] = 0
        V2 = view([2, CT, H, VW]); pexp2 = view([4, 2, S]); oT2 = view([2, S]); mrow2 = view([2, S], BF16)
        cmax2 = view([H, TB]); nm2 = view([HH, TB]); nr2 = view([HH, TB]); rl2 = view([TB, HG, 1])
        nmb2 = view([TB, P // HH, HH], BF16)
        at[0] = max(at[0], yg_at + NT * D)
        q2_at = at[0]
        Q2 = view([2, H, S], BF16)
        k2_at = at[0]
        K2 = view([2, H, CH], BF16)
        at[0] = small_at = max(at[0], part3_end)
        qr = view([KC, S]); qp = view([2, 3, KC, S], BF16)
        at[0] = q_at
        hot_s = view([NY]); dist_s = view([NY]); dist_g = view([NY])
        assert at[0] <= v_at
        at[0] = small_at
        wp1 = view([KC, NAV]); wp2 = view([E]); bp1 = view([1]); bp2 = view([E])
        wof = view([KC, D]); bo_s = view([D])
        nav = view([B]); al = view([2, 8, E]); sel_i = view([2], I32)
        p_b1 = view([B, FC]); p_b2 = view([B, KC])
        p_w1 = view([B, KC, F], off=q2_at); p_w2 = view([B, FC, D], off=k2_at)
        assert B * KC * F <= H * S // 2 and B * FC * D <= H * CH // 2
        o_s = view([NT, D], off=q2_at + H * S // 2)
        assert NT * D <= H * S // 2
        hT = view([2, FC, S], off=0); rT = view([2, KC, S])
        assert at[0] <= q2_at

        ps = ctx.enter_context(nc.psum_tensor("ps", [P, 8, 512], F32))

        s_const = sem("const_loaded")
        s_cand = sem("candidates_loaded")
        s_x = [sem(f"x_loaded{b}") for b in range(B)]
        s_ctxT = [sem(f"ctxT_loaded{i}") for i in range(2)]
        s_ctxN = [sem(f"ctxN_loaded{i}") for i in range(2)]
        s_wts = sem("weights_loaded")
        s_w12 = sem("expert_weights_loaded")
        s_bconst = sem("bf16_constants")
        s_dv = sem("vector_steps")
        s_ln = sem("layer_norm_done")
        s_lnst = sem("layer_norm_roots")
        s_tpr = sem("transposed")
        s_tpf = sem("transpose_taken")
        s_h = sem("hidden_product")
        s_a = sem("hidden_activated")
        s_mm2 = sem("hidden_used")
        s_res = sem("residual_added")
        s_soft = sem("router_shifted")
        s_exp8 = sem("router_exp")
        s_ge = sem("candidates_compared")
        s_cnt = sem("candidates_counted")
        s_gq = sem("router_masks")
        s_gp = sem("router_prefixes")
        s_slot = sem("slots_known")
        s_zero = sem("slots_zeroed")
        s_zt = sem("zero_tile")
        s_scat = sem("tokens_scattered")
        s_xsb = sem("block_loaded")
        s_xsTr = sem("block_transposed")
        s_xsT = sem("block_transpose_taken")
        s_eh = sem("expert_hidden")
        s_ea = sem("expert_activated")
        s_et = sem("expert_hidden_transposed")
        s_etc = sem("expert_transpose_taken")
        s_ey = sem("expert_answer")
        s_eyc = sem("expert_answer_taken")
        s_ys = sem("answers_stored")
        s_ysd = sem("all_answers_stored")
        s_gat = [sem(f"answers_gathered{b}") for b in range(B)]
        s_mask = sem("mask_loaded")
        s_mk = sem("mask_any")
        s_mkp = sem("mask_any_by_batch")
        s_mk2 = sem("mask_active")
        s_lrow = sem("active_row")
        s_list = sem("chunk_list")
        s_mrow = sem("mask_row_made")
        s_mst = sem("mask_rows_stored")
        s_dp = sem("distance_product")
        s_dpc = sem("distance_taken")
        s_dst = sem("distances_made")
        s_dstore = sem("distances_stored")
        s_hot = sem("distance_table_loaded")
        s_init3 = sem("attention_buffers_set")
        s_q = sem("q_product")
        s_qp = sem("q_parts_made")
        s_qst = [sem(f"q_parts_stored{i}") for i in range(2)]
        s_cc = sem("chunk_loaded")
        s_kpr = sem("k_product")
        s_vpr = sem("v_product")
        s_k1 = sem("k_first_part")
        s_kp = sem("k_parts_made")
        s_kst = sem("k_parts_stored")
        s_vt = sem("v_taken")
        s_kq = sem("k_q_rows_loaded")
        s_hk = sem("distance_window_loaded")
        s_dvr = sem("vector_steps_of_a_round")
        s_dvm = sem("chunk_weighted")
        s_rows = sem("constant_rows_set")
        s_dv3 = sem("vector_steps_of_a_chunk")
        s_dtake = sem("distance_buffers_free")
        s_sc = sem("scores_for_max")
        s_scu = sem("scores_for_max_taken")
        s_nm = sem("max_split")
        s_nmt = sem("max_transposed")
        s_nmc = sem("max_rows_made")
        s_mr = sem("max_rows_loaded")
        s_st = sem("scores")
        s_pe = sem("probs")
        s_pv = sem("probs_used")
        s_oc = sem("values_taken")
        s_ot = sem("values_transposed")
        s_ou = sem("values_merged")
        s_wgt = sem("merge_weights_shifted")
        s_wge = sem("merge_weights")
        s_acc_f = sem("attention_normalised")
        s_pj = sem("projected")
        s_w4 = sem("part4_weights_loaded")
        s_nv = sem("router4_product")
        s_nva = sem("router4_activated")
        s_nl = sem("router4_logits")
        s_l4 = sem("router4_shifted")
        s_e4 = sem("router4_exp")
        s_sel = sem("expert4_known")
        s_pw = [sem(f"expert4_loaded{b}") for b in range(B)]
        s_p4 = sem("part4_hidden")
        s_p4a = sem("part4_activated")
        s_p4u = sem("part4_hidden_used")
        s_rt = sem("part4_reasoned")
        s_rtc = sem("part4_reasoned_taken")
        s_po = sem("part4_out")
        s_fo = sem("final_rows")
        s_ctxe = [sem(f"last_keys_loaded{i}") for i in range(2)]
        s_ekv = sem("last_kv_product")
        s_ek1 = sem("last_k_first_part")
        s_ekr = sem("last_k_rest")
        s_ekp = sem("last_k_parts_made")
        s_ev = sem("last_v_taken")
        s_evi = sem("last_v_buffers_set")
        s_ekst = sem("last_k_stored")
        s_evst = [sem(f"last_v_stored{i}") for i in range(2)]
        s_moe = sem("experts_added")
        s_expd = sem("experts_done")
        s_q1 = sem("q_first_part")
        s_qr = sem("q_rest")
        f_ones = sem("constant_rows_loaded")
        f_rows = [[sem(f"rows_loaded_slot{i}_half{j}") for j in range(2)] for i in range(2)]
        f_v = [sem(f"values_loaded_slot{i}") for i in range(2)]
        f_sc = sem("scores_for_max_fast")
        f_scu = sem("scores_for_max_fast_taken")
        f_nm = sem("max_split_fast")
        f_mr = [sem(f"max_rows_fast_loaded{i}") for i in range(2)]
        f_st = sem("scores_fast")
        f_pe = sem("probs_fast")
        f_pv = sem("probs_fast_used")
        f_oc = sem("values_fast_taken")
        f_ot = sem("values_fast_transposed")
        f_ou = sem("values_fast_normalised")
        f_dv = sem("vector_steps_of_attention")
        s_out = sem("rows_stored")

        def per(i, k):
            return i * k

        block = ctx.enter_context(nc.Block())

        @block.sync
        def _(sp):
            for s_free in (s_ys, s_kst, s_mr):
                sp.sem_inc(s_free, 1)
            sp.dma_start(x_tok[:, 0:TB, :], a["x"][0:S, :].rearrange("(t p) d -> p t d", p=P)).then_inc(s_x[0], 16)
            sp.dma_start(cst[:, :], a["c_f32"]).then_inc(s_const, 16)

            def load_ctx(b):
                if b >= 2:
                    sp.wait_ge(s_mm2, NF * (b - 1))
                sp.dma_start(ctxT_s[:, b % 2, :, :], a["ctxT"][b].rearrange("(k p) n -> p k n", p=P)[:, :, 0:NF * P]).then_inc(s_ctxT[b % 2], 16)
                sp.dma_start(ctxN_s[:, b % 2, :, :], a["ctxN"][b].rearrange("(f p) d -> p f d", p=P)).then_inc(s_ctxN[b % 2], 16)

            load_ctx(0)
            for b in range(1, B):
                sp.dma_start(x_tok[:, TB * b:TB * b + TB, :],
                             a["x"][S * b:S * b + S, :].rearrange("(t p) d -> p t d", p=P)).then_inc(s_x[b], 16)
            sp.dma_start(cand_c[:, :], a["c_cand"]).then_inc(s_cand, 16)
            sp.dma_start(wg[:, :, :], a["Wg"].rearrange("(k p) e -> p k e", p=P)).then_inc(s_wts, 16)
            load_ctx(1)
            sp.dma_start(mask4[:, :], a["mask"]).then_inc(s_mask, 16)
            sp.dma_start(maskw[:, 0, :], a["c_real"]).then_inc(s_mask, 16)
            sp.dma_start(relb[:, :], a["rel_biasT"]).then_inc(s_mask, 16)
            for w, name in ((wq, "WqT"), (wk, "WkT"), (wv, "WvT"), (wo, "WoT")):
                sp.dma_start(w[:, :, :], a[name].rearrange("(k p) n -> p k n", p=P)).then_inc(s_wts, 16)
            for e in range(E):
                sp.dma_start(w1_s[:, e, :, :], a["W1"][e].rearrange("(k p) f -> p k f", p=P)).then_inc(s_w12, 16)
                sp.dma_start(w2_s[:, e, :, :], a["W2"][e].rearrange("(f p) d -> p f d", p=P)).then_inc(s_w12, 16)
            load_ctx(2)
            load_ctx(3)
            sp.wait_ge(s_zt, 1)
            sp.dma_start(xs_d.rearrange("(j p) d -> p j d", p=P),
                         zero_t[:, :].unsqueeze(1).broadcast_to([P, NBLK + 2, D])).then_inc(s_zero, 16)
            sp.dma_start(ys_d.rearrange("(j p) d -> p j d", p=P),
                         zero_t[:, :].unsqueeze(1).broadcast_to([P, NBLK, D])).then_inc(s_zero, 16)
            sp.wait_ge(s_cnt, 1)

            def load_last(b):
                sp.dma_start(ctx_e[:, b % 2, :, :], a["ctxT"][b].rearrange("(k p) n -> p k n", p=P)[:, :, 0:CH]).then_inc(s_ctxe[b % 2], 16)

            load_last(0)
            load_last(1)

            def store_keys(b):
                sp.wait_ge(s_ekp, KC * (b + 1))
                for m in range(KC):
                    for t in range(3):
                        sp.dma_start(k0_d[b, t, :, m * HH:m * HH + HH, :].rearrange("d h n -> h d n"), kp_e[:, t, m, :]).then_inc(s_ekst, 16)

            def store_values(b):
                sp.wait_ge(s_ev, 2 * (b + 1))
                sp.dma_start(v0_d[b], v_e[b // 2][:, b % 2, :, :, :].rearrange("p t h d -> p (t h d)")).then_inc(s_evst[b % 2], 16)

            store_keys(0)
            sp.wait_ge(s_mrow, 1)
            sp.dma_start(mask_d, mrow_b[:, :]).then_inc(s_mst, 16)
            sp.wait_ge(s_slot, 2)
            pairs = sp.value_load(be_i[0:1, NBLK:NBLK + 1], min_val=1, max_val=PAIRS)
            sp.wait_ge(s_zero, 32)
            sp.wait_ge(s_scat, 16 * NT)

            def load_block(i):
                sp.dma_start(xsb[:, :, :], xs_d.rearrange("(i j p) d -> i p j d", p=P, j=2)[i]).then_inc(s_xsb, 16)

            load_block(0)
            for b in range(2):
                if b >= 1:
                    store_keys(b)
                store_values(b)
                sp.wait_ge(s_ekv, 4 * (b + 1))
                load_last(b + 2)
            with sp.Fori(0, pairs) as i:
                sp.wait_ge(s_xsTr, i * 2 + 2)
                sp.dma_start(xsb[:, :, :], xs_d.rearrange("(i j p) d -> i p j d", p=P, j=2)[bass.ds(i + 1, 1)]
                             .rearrange("i p j d -> (i p) j d")).then_inc(s_xsb, 16)
                sp.wait_ge(s_eyc, i * 2 + 2)
                sp.dma_start(ys_d.rearrange("(i j p) d -> i p j d", p=P, j=2)[bass.ds(i, 1)]
                             .rearrange("i p j d -> (i p) j d"), y_s[:, :, :]).then_inc(s_ys, 16)
            sp.wait_ge(s_ys, pairs * 16 + 1)
            sp.sem_inc(s_ysd, 1)
            for b in range(2, B):
                store_keys(b)
                store_values(b)
            sp.wait_ge(s_list, 1)
            near = sp.value_load(lst_i[0:1, 33:34], min_val=0, max_val=NC - 1)

            def store_queries(b):
                sp.wait_ge(s_qp, KC * (b + 1))
                for h in range(KC):
                    for t in range(3):
                        sp.dma_start(q_d[b, t, :, h * HH:h * HH + HH, :].rearrange("d h n -> h d n"),
                                     qp[:, b % 2, t, h, :]).then_inc(s_qst[b % 2], 16)

            def router_weights():
                for i in range(2):
                    sp.wait_ge(s_qst[i], 48 * KC * B // 2)
                sp.dma_start(wp1[:, :, :], a["Wp1"].rearrange("(k p) n -> p k n", p=P)).then_inc(s_w4, 16)
                sp.dma_start(wp2[:, :], a["Wp2"]).then_inc(s_w4, 16)
                sp.dma_start(bp1[:, :], a["bp1"].unsqueeze(1)).then_inc(s_w4, 16)
                sp.dma_start(bp2[0:B, :], a["bp2"].unsqueeze(0).broadcast_to([B, E])).then_inc(s_w4, 16)
                sp.dma_start(wof[:, :, :], a["Wof"].rearrange("(k p) n -> p k n", p=P)).then_inc(s_w4, 16)
                sp.dma_start(bo_s[:, :], a["bo"].unsqueeze(0).broadcast_to([P, D])).then_inc(s_w4, 16)

            def general_way():
                for b in range(B):
                    store_queries(b)
                sp.wait_ge(s_moe, B)
                sp.wait_ge(s_init3, 1)
                sp.dma_start(hot_s[0:BUCKETS, :], a["c_hot"]).then_inc(s_hot, 16)
                for b in range(B):
                    sp.wait_ge(s_dst, b + 1)
                    sp.dma_start(dist_d[b], dist_g[0:H, :]).then_inc(s_dstore, 16)
                n = sp.value_load(lst_i[0:1, 32:33], min_val=1, max_val=B * NC)
                sp.wait_ge(s_rows, 1)
                for i in range(2):
                    sp.wait_ge(s_qst[i], 48 * KC * B // 2)
                sp.wait_ge(s_mst, 16)
                sp.wait_ge(s_dstore, 16 * B)
                with sp.Fori(0, n) as i:
                    bi = sp.value_load(lst_i[0:1, bass.ds(i, 1)], min_val=0, max_val=B - 1)
                    ci = sp.value_load(lst_i[0:1, bass.ds(i + 16, 1)], min_val=0, max_val=NC - 1)
                    sp.wait_ge(s_vpr, i + 1)
                    sp.dma_start(ctx_c[:, :, :], a["ctxT"][bass.ds(bi, 1), :, bass.ds(ci * CH, CH)]
                                 .rearrange("b (k p) n -> p (b k) n", p=P)).then_inc(s_cc, 16)
                    sp.wait_ge(s_pv, i * (NG * CT) + 1)
                    qv = q_d[bass.ds(bi, 1)].rearrange("b t d h n -> (b t) d h n")
                    for r, part, reps in ((0, 0, 3), (3, 1, 2), (5, 2, 1)):
                        for k in range(reps):
                            sp.dma_start(Q[(r + k) * DK:(r + k + 1) * DK, :, :], qv[part]).then_inc(s_kq, 16)
                    sp.dma_start(K[ROW_MASK:ROW_MASK + 1, :, :],
                                 mask_d[bass.ds(bi * NC + ci, 1), :].unsqueeze(1).broadcast_to([1, H, CH])).then_inc(s_kq, 16)
                    sp.wait_ge(s_kp, i + 1)
                    for h in range(KC):
                        sp.dma_start(k_d.rearrange("t (k p) n -> p t k n", p=P)[:, :, h, :], kp[:, :, h, :]).then_inc(s_kst, 16)
                    sp.wait_ge(s_kst, (i + 1) * (16 * KC) + 1)
                    kv = k_d.rearrange("t (h d) n -> t d h n", d=DK)
                    for r, part in enumerate((0, 1, 2, 0, 1, 0)):
                        sp.dma_start(K[r * DK:(r + 1) * DK, :, :], kv[part]).then_inc(s_kq, 16)
                    dv = bass.AP(dist_d.tensor, 0, [[H * NY, B], [NY, H], [1, P], [1, NY - P + 1]])

                    def window(g):
                        sp.dma_start(Hk[:, :, :], dv[bass.ds(bi, 1), HG * g:HG * g + HG, :, bass.ds(ci * CH, HW_)]
                                     .rearrange("b h k x -> k (b h) x")).then_inc(s_hk, 16)

                    with sp.If(ci > 0):
                        for g in range(NG):
                            sp.wait_ge(s_scu, i * (H * TB // 2) + g * (HG * TB // 2) + 1)
                            window(g)
                    with sp.Else():
                        sp.sem_inc(s_hk, 16 * NG)
                    sp.wait_ge(s_nmc, i + 1)
                    for t in range(3):
                        sp.dma_start(Q[ROW_MAX + t:ROW_MAX + t + 1, :, :], mrow[t * H:(t + 1) * H, :]).then_inc(s_mr, 16)
                    with sp.If(ci > 0):
                        for g in range(NG):
                            sp.wait_ge(s_pv, i * (NG * CT) + g * CT + 1)
                            window(g)
                    with sp.Else():
                        sp.sem_inc(s_hk, 16 * NG)
                sp.wait_ge(s_acc_f, B)
                router_weights()

            def fast_way():
                def keys(b, half):
                    i, hs = b % 2, slice(half * HH, half * HH + HH)
                    if b >= 2:
                        sp.wait_ge(f_pv, NG * CT * (b - 2) + NG * CT // 2 * (half + 1))
                    kv = k0_d[b, :, :, hs, :].rearrange("t d h n -> (t d) (h n)")
                    for r, n in ((0, 3), (3, 2), (5, 1)):
                        sp.dma_start(K2[r * DK:(r + n) * DK, i, hs, :], kv[0:n * DK]).then_inc(f_rows[i][half], 16)
                    sp.dma_start(K2[ROW_MASK:ROW_MASK + 1, i, hs, :],
                                 mask_d[b * NC:b * NC + 1, :].unsqueeze(1).broadcast_to([1, HH, CH])).then_inc(f_rows[i][half], 16)

                def queries(b, half):
                    i, hs = b % 2, slice(half * HH, half * HH + HH)
                    if half == 0:
                        sp.wait_ge(s_qst[i], 48 * KC * (b // 2 + 1))
                    qv = q_d[b, :, :, hs, :].rearrange("t d h n -> t d (h n)")
                    for r, n in ((0, 3), (3, 2), (5, 1)):
                        sp.dma_start(Q2[r * DK:(r + n) * DK, i, hs, :],
                                     qv[3 - n].unsqueeze(0).broadcast_to([n, DK, HH * S])).then_inc(f_rows[i][half], 16)

                def values(b):
                    if b >= 2:
                        sp.wait_ge(f_pv, NG * CT * (b - 1))
                    else:
                        sp.wait_ge(s_moe, B)
                    sp.dma_start(V2[:, b % 2, :, :, :].rearrange("p t h d -> p (t h d)"), v0_d[b]).then_inc(f_v[b % 2], 16)

                def max_rows(b, half):
                    sp.wait_ge(f_scu, APB * b + (A_T0 if half == 0 else A_T1) + 1)
                    for t in range(3):
                        sp.dma_start(Q2[ROW_MAX + t:ROW_MAX + t + 1, b % 2, half * HH:half * HH + HH, :],
                                     mrow2[t * HH:(t + 1) * HH, half, :]).then_inc(f_mr[half], 16)

                for i in range(2):
                    sp.dma_start(Q2[ROW_MASK:ROW_MASK + 1, i, :, :].rearrange("p h (c n) -> p (h c) n", n=P),
                                 ones_b[0:1, :].unsqueeze(1).broadcast_to([1, H * S // P, P])).then_inc(f_ones, 16)
                    sp.dma_start(K2[ROW_MAX:ROW_MAX + 3, i, :, :].rearrange("p h (c n) -> p (h c) n", n=P),
                                 ones_b[0:3, :].unsqueeze(1).broadcast_to([3, H * CH // P, P])).then_inc(f_ones, 16)
                for b in range(2):
                    for half in range(2):
                        keys(b, half)
                for b in range(2):
                    store_queries(b)
                    for half in range(2):
                        queries(b, half)
                values(0)
                values(1)
                store_queries(2)
                store_queries(3)
                max_rows(0, 0)
                max_rows(0, 1)
                for b in range(B):
                    if b + 1 < B:
                        max_rows(b + 1, 0)
                    if b == B - 2:
                        router_weights()
                    if b + 2 < B:
                        for half in range(2):
                            keys(b + 2, half)
                            queries(b + 2, half)
                        values(b + 2)
                    if b + 1 < B:
                        max_rows(b + 1, 1)

            sp.wait_ge(s_ekst, 48 * KC * B)
            for i in range(2):
                sp.wait_ge(s_evst[i], 16 * B // 2)
            sp.wait_ge(s_expd, 1)
            sp.wait_ge(s_mst, 16)
            with sp.If(near > 0):
                general_way()
            with sp.Else():
                fast_way()
            def expert(b, row, col):
                e = sp.value_load(sel_i[row:row + 1, col:col + 1], min_val=0, max_val=E - 1)
                sp.dma_start(p_w1[:, b, :, :], a["pW1"][bass.ds(e, 1)].rearrange("e (k p) f -> p (e k) f", p=P)).then_inc(s_pw[b], 16)
                sp.dma_start(p_b1[:, b, :], a["pb1"][bass.ds(e, 1)].rearrange("e (f p) -> p (e f)", p=P),
                             allow_slow_non_contiguous=True).then_inc(s_pw[b], 16)
                sp.dma_start(p_w2[:, b, :, :], a["pW2"][bass.ds(e, 1)].rearrange("e (f p) d -> p (e f) d", p=P)).then_inc(s_pw[b], 16)
                sp.dma_start(p_b2[:, b, :], a["pb2"][bass.ds(e, 1)].rearrange("e (k p) -> p (e k)", p=P),
                             allow_slow_non_contiguous=True).then_inc(s_pw[b], 16)

            sp.wait_ge(s_sel, 1)
            sp.wait_ge(s_acc_f, B - 1)
            for b in range(B - 1):
                expert(b, b, 0)
            sp.wait_ge(s_sel, 2)
            expert(B - 1, 0, 1)
            for b in range(B):
                sp.wait_ge(s_fo, b + 1)
                sp.dma_start(a["out"][S * b:S * b + S, :].rearrange("(t p) d -> p t d", p=P),
                             o_s[:, TB * b:TB * b + TB, :]).then_inc(s_out, 16)
            sp.wait_ge(s_out, 16 * B)

        @block.tensor
        def _(pe):
            for s_free in (s_vpr, s_pv):
                pe.sem_inc(s_free, 1)
            tp = [0]

            def tp_bank(first=6):
                if tp[0] >= 2:
                    pe.wait_ge(s_tpf, tp[0] - 1)
                bank = first + tp[0] % 2
                tp[0] += 1
                return ps[:, bank, :]

            def transposes(src, b, bank=6):
                for k in range(KC):
                    o = tp_bank(bank)
                    for t in range(TB):
                        ins = pe.transpose(o[:, t * P:t * P + P], src[:, TB * b + t, k * P:k * P + P], eye)
                    ins.then_inc(s_tpr, 1)

            pe.wait_ge(s_const, 16)
            pe.wait_ge(s_ln, 1)
            transposes(xn, 0)
            NK = B * NF

            def logits(b):
                pe.wait_ge(s_tpf, tp[0])
                o = tp_bank()
                for t in range(TB):
                    for k in range(KC):
                        ins = pe.matmul(o[:, t * E:t * E + E], xnT[:, k, S * b + t * P:S * b + t * P + P], wg[:, k, :],
                                        start=(k == 0), stop=(k == KC - 1))
                ins.then_inc(s_tpr, 1)

            for k in range(NK + 2):
                if k < NK:
                    b, f = divmod(k, NF)
                    if f == 0:
                        pe.wait_ge(s_ctxT[b % 2], 16 * (b // 2 + 1))
                        pe.wait_ge(s_tpf, KC * (b + 1) if b < 3 else KC * 4)
                    if k >= 2:
                        pe.wait_ge(s_a, k - 1)
                    for c in range(KC):
                        ins = pe.matmul(ps[:, 4 + k % 2, :], ctxT_s[:, b % 2, c, f * P:f * P + P], xnT[:, c, S * b:S * b + S],
                                        start=(c == 0), stop=(c == KC - 1))
                    ins.then_inc(s_h, 1)
                if k >= 2:
                    b, f = divmod(k - 2, NF)
                    if f == 0:
                        pe.wait_ge(s_ctxN[b % 2], 16 * (b // 2 + 1))
                        if b >= 2:
                            pe.wait_ge(s_res, b - 1)
                    pe.wait_ge(s_a, k - 1)
                    for t in range(TB):
                        ins = pe.matmul(ps[:, b % 2 * 2 + t // 2, t % 2 * D:t % 2 * D + D], hid[:, (k - 2) % 4, t * P:t * P + P], ctxN_s[:, b % 2, f, :],
                                        start=(f == 0 and t % 2 == 0), stop=(f == NF - 1), skip_group_check=True)
                    ins.then_inc(s_mm2, 1)
                if k == 5:
                    pe.wait_ge(s_ln, 2)
                    transposes(xn, 1)
                if k == 12:
                    pe.wait_ge(s_ln, 3)
                    transposes(xn, 2)
                if k == 20:
                    pe.wait_ge(s_ln, 4)
                    transposes(xn, 3)
                if k == 25:
                    pe.wait_ge(s_wts, 16 * 5)
                    pe.wait_ge(s_ln, 5)
                    transposes(xn, 0)
                    logits(0)
                if k == 38:
                    pe.wait_ge(s_ln, 6)
                    transposes(xn, 1)
                    logits(1)
                if k == 47:
                    pe.wait_ge(s_ln, 7)
                    transposes(xn, 2)
                    logits(2)
            for b in range(3, 4):
                pe.wait_ge(s_ln, 5 + b)
                transposes(xn, b)
                logits(b)
            pe.wait_ge(s_bconst, 1)
            with pe.Fori(0, ROUNDS // 2) as two:
                for j in range(2):
                    pe.wait_ge(s_ge, two * 2 + j + 1)
                    for t in range(NT):
                        ins = pe.matmul(ps[:, 0, 0:CAND * E], ones_b[:, :], ge_b[:, :, t, :], start=(t == 0), stop=(t == NT - 1))
                    ins.then_inc(s_cnt, 1)

            def prefix(dst, src):
                pe.matmul(dst, tri_b[:, :], src, start=True, stop=True, skip_group_check=True)
                for t in range(NT - 1):
                    n = NT - 1 - t
                    ins = pe.matmul(dst[:, (t + 1) * E:], ones_b[:, :], src[:, t, :].unsqueeze(1).broadcast_to([P, n, E]),
                                    start=False, stop=True, skip_group_check=True)
                return ins

            def total(dst, src):
                for t in range(NT):
                    ins = pe.matmul(dst, ones_b[:, :], src[:, t, :], start=(t == 0), stop=(t == NT - 1))
                return ins

            pe.wait_ge(s_gq, 1)
            prefix(ps[:, 1, 0:NT * E], eq_b)
            total(ps[:, 2, 0:E], gt).then_inc(s_gp, 1)
            pe.wait_ge(s_gq, 2)
            prefix(ps[:, 3, 0:NT * E], hot_b)
            total(ps[:, 4, 0:E], hot_b).then_inc(s_gp, 1)

            def last_keys(b):
                pe.wait_ge(s_ctxe[b % 2], 16 * (b // 2 + 1))
                for u in range(4):
                    bank = ps[:, 5 * (u % 2), :]
                    if u >= 2:
                        pe.wait_ge(s_ekr, KC * b + u - 1)
                    elif b >= 1:
                        pe.wait_ge(s_ev, 2 * (b - 1) + u + 1)
                    for k in range(KC):
                        if u < KC:
                            ins = pe.matmul(bank, wk[:, k, u * P:u * P + P], ctx_e[:, b % 2, k, :], start=(k == 0), stop=(k == KC - 1))
                    for t in range(2 if u >= KC else 0):
                        for k in range(KC):
                            tt = 2 * (u - KC) + t
                            ins = pe.matmul(bank[:, t * D:t * D + D], ctx_e[:, b % 2, k, tt * P:tt * P + P], wv[:, k, :],
                                            start=(k == 0), stop=(k == KC - 1))
                    ins.then_inc(s_ekv, 1)

            pe.wait_ge(s_mk, 1)
            pe.matmul(ps[0:B * NC, 6, 0:1], cst[0:B * NC, C_BLK:C_BLK + 16], msm[:, 0:1], start=True, stop=True)
            pe.matmul(ps[:, 7, 0:B], msm[:, 0:1].broadcast_to([B * NC, P]), cst[0:B * NC, C_BLK + 16:C_BLK + 16 + B],
                      start=True, stop=True).then_inc(s_mkp, 1)
            last_keys(0)
            pe.wait_ge(s_mk2, 1)
            pe.matmul(ps[0:1, 6, 0:16], msm[:, 3:4], cst[0:B * NC, C_EYE:C_EYE + 16], start=True, stop=True).then_inc(s_lrow, 1)
            last_keys(1)
            pe.wait_ge(s_list, 1)
            pe.wait_ge(s_ev, 2 * 2)

            def block_transposes():
                for j in range(2):
                    for k in range(KC):
                        ins = pe.transpose(ps[:, 6 + j, k * P:k * P + P], xsb[:, j, k * P:k * P + P], eye)
                    ins.then_inc(s_xsTr, 1)

            pe.wait_ge(s_slot, 2)
            pairs = pe.value_load(be_i[0:1, NBLK:NBLK + 1], min_val=1, max_val=PAIRS)
            pe.wait_ge(s_w12, 16 * 2 * E)
            pe.wait_ge(s_xsb, 16)
            block_transposes()
            with pe.Fori(0, pairs) as i:
                place = [pe.value_load(be_i[0:1, bass.ds(i * 2 + j, 1)], min_val=0, max_val=(E - 1) * KC * F) for j in range(2)]
                pe.wait_ge(s_xsT, i * 2 + 2)
                for j in range(2):
                    for k in range(KC):
                        ins = pe.matmul(ps[:, j, :], xsT[:, j, k, :],
                                        w1_s.rearrange("p e k f -> p (e k f)")[:, bass.ds(place[j] + k * F, F)],
                                        start=(k == 0), stop=(k == KC - 1))
                    ins.then_inc(s_eh, 1)
                for j in range(2):
                    pe.wait_ge(s_ea, i * 2 + j + 1)
                    for f in range(FC):
                        ins = pe.transpose(ps[:, 2 + j, f * P:f * P + P], hexp[:, j, f * P:f * P + P], eye)
                    ins.then_inc(s_et, 1)
                    if j == 0:
                        pe.wait_ge(s_xsb, (i + 2) * 16)
                        block_transposes()
                for j in range(2):
                    pe.wait_ge(s_etc, i * 2 + j + 1)
                    for f in range(FC):
                        ins = pe.matmul(ps[:, 4 + j, 0:D], hexpT[:, j, f, :],
                                        w2_s.rearrange("p e f d -> p (e f d)")[:, bass.ds(place[j] + f * D, D)],
                                        start=(f == 0), stop=(f == FC - 1))
                    ins.then_inc(s_ey, 1)
            pe.wait_ge(s_expd, 1)
            pe.wait_ge(s_xsT, pairs * 2 + 2)
            for b in range(2, B):
                last_keys(b)
            pe.wait_ge(s_ev, 2 * B)

            pe.wait_ge(s_list, 1)
            near = pe.value_load(lst_i[0:1, 33:34], min_val=0, max_val=NC - 1)

            def turn_queries(b):
                pe.wait_ge(s_ln, 2 * B + b + 1)
                transposes(xn, b)

            def queries(b, beside=None):
                pe.wait_ge(s_tpf, tp[0])
                for m in range(KC):
                    if b >= 1:
                        pe.wait_ge(s_qr, KC * (b - 1) + m + 1)
                    for k in range(KC):
                        ins = pe.matmul(ps[:, 2 + m, :], wq[:, k, m * P:m * P + P], xnT[:, k, S * b:S * b + S],
                                        start=(k == 0), stop=(k == KC - 1))
                        if k == KC - 1:
                            ins.then_inc(s_q, 1)
                        if beside is not None:
                            beside(KC * m + k)

            def turn(b, bank=6):
                pe.wait_ge(s_acc_f, b + 1)
                if b >= 1:
                    pe.wait_ge(s_res, B + b)
                transposes(xn, b, bank)

            def project(b):
                pe.wait_ge(s_tpf, tp[0])
                for t in range(TB):
                    for k in range(KC):
                        ins = pe.matmul(ps[:, t // 2, t % 2 * D:t % 2 * D + D], xnT[:, k, S * b + t * P:S * b + t * P + P], wo[:, k, :],
                                        start=(k == 0), stop=(k == KC - 1))
                ins.then_inc(s_pj, 1)

            def turn4(b, bank=6):
                pe.wait_ge(s_ln, 3 * B + b + 1)
                pe.wait_ge(s_res, B + b + 1)
                transposes(xn, b, bank)

            def route(lo, hi, i):
                pe.wait_ge(s_tpf, tp[0])
                pe.wait_ge(s_w4, 16 * 6)
                if i >= 1:
                    pe.wait_ge(s_l4, i)
                for k in range(KC):
                    ins = pe.matmul(ps[:, 0, 0:hi - lo], wp1[:, k, :], xnT[:, k, S * lo + S - 1:S * hi:S], start=(k == 0), stop=(k == KC - 1))
                ins.then_inc(s_nv, 1)

            def route_logits(lo, hi, i):
                pe.wait_ge(s_nva, i + 1)
                pe.matmul(ps[0:hi - lo, 1, 0:E], nav[:, lo:hi], wp2[:, :], start=True, stop=True).then_inc(s_nl, 1)

            tp_before = tp[0]

            def general_way():
                for b in range(B):
                    turn_queries(b)
                    queries(b)
                pe.wait_ge(s_qr, KC * B)
                pe.wait_ge(s_hot, 16)
                for j in range(NY // 512):
                    pe.matmul(ps[0:H, 3 + j, :], relb[:, :], hot_s[0:BUCKETS, j * 512:j * 512 + 512], start=True, stop=True).then_inc(s_dp, 1)
                pe.wait_ge(s_dpc, NY // 512)
                n = pe.value_load(lst_i[0:1, 32:33], min_val=1, max_val=B * NC)
                SPB = H * TB // 2
                EPB = CT * H // 2
                with pe.Fori(0, n) as i:
                    ci = pe.value_load(lst_i[0:1, bass.ds(i + 16, 1)], min_val=0, max_val=NC - 1)
                    pe.wait_ge(s_cc, (i + 1) * 16)
                    pe.wait_ge(s_pe, i * EPB + 1)
                    for m in range(KC):
                        for k in range(KC):
                            ins = pe.matmul(ps[:, m, :], wk[:, k, m * P:m * P + P], ctx_c[:, k, :], start=(k == 0), stop=(k == KC - 1))
                    ins.then_inc(s_kpr, 1)
                    for t in range(CT):
                        for k in range(KC):
                            ins = pe.matmul(ps[:, 2 + t // 2, (t % 2) * D:(t % 2) * D + D], ctx_c[:, k, t * P:t * P + P], wv[:, k, :],
                                            start=(k == 0), stop=(k == KC - 1))
                    ins.then_inc(s_vpr, 1)
                    pe.wait_ge(s_kq, (i + 1) * (16 * 13))
                    pe.wait_ge(s_kp, i + 1)
                    pe.wait_ge(s_vt, i + 1)
                    def scores_for_max(near):
                        for h in range(H):
                            if near and h % HG == 0:
                                pe.wait_ge(s_hk, i * (2 * 16 * NG) + (h // HG + 1) * 16)
                            for jp in range(TB // 2):
                                u = h * (TB // 2) + jp
                                pe.wait_ge(s_scu, i * SPB + max(u - 1, 0) + 1)
                                for j in range(2):
                                    ins = pe.matmul(ps[:, 2 * (u % 2) + j, :], Q[0:KR + 1, h, (2 * jp + j) * P:(2 * jp + j + 1) * P],
                                                    K[0:KR + 1, h, :], start=True, stop=True, skip_group_check=True)
                                    for t in range(CT if near else 0):
                                        x = t * P + (2 * jp + j) * P
                                        ins = pe.matmul(ps[:, 2 * (u % 2) + j, t * P:t * P + P], Hk[:, h % HG, x:x + P], eye,
                                                        start=False, stop=True, skip_group_check=True)
                                ins.then_inc(s_sc, 1)

                    with pe.If(ci > 0):
                        scores_for_max(True)
                    with pe.Else():
                        scores_for_max(False)
                    pe.wait_ge(s_nm, i + 1)
                    mt = ps[:, 7, 0:256].bitcast(BF16)
                    for j in range(TB):
                        ins = pe.transpose(mt[:, j * P:j * P + P], nmb[:, j, :, :].rearrange("p t h -> p (t h)"), eye_b[:, :])
                    ins.then_inc(s_nmt, 1)
                    pe.wait_ge(s_mr, (i + 1) * 48 + 1)
                    def attend(near):
                        for g in range(NG):
                            if near:
                                pe.wait_ge(s_hk, i * (2 * 16 * NG) + (NG + g + 1) * 16)
                            for t in range(CT + 1):
                                for hp in range(HG // 2 if t < CT else 0):
                                    u = (g * CT + t) * 2 + hp
                                    pe.wait_ge(s_pe, i * EPB + max(u - 1, 0) + 1)
                                    for j in range(2):
                                        h = g * HG + hp * 2 + j
                                        ins = pe.matmul(ps[:, 2 * (u % 2) + j, :], K[0:KROWS, h, t * P:t * P + P], Q[0:KROWS, h, :],
                                                        start=True, stop=True, skip_group_check=True)
                                        if near:
                                            ins = pe.matmul(ps[:, 2 * (u % 2) + j, :], eye, Hk[:, hp * 2 + j, t * P:t * P + S],
                                                            start=False, stop=True, skip_group_check=True)
                                    ins.then_inc(s_st, 1)
                                if t >= 1:
                                    u = (g * CT + t - 1) * 2
                                    pe.wait_ge(s_pe, i * EPB + u + 2 + 1)
                                    if t == 1:
                                        pe.wait_ge(s_oc, i * NG + g + 1)
                                    for j in range(HG):
                                        ins = pe.matmul(ps[VW * j:VW * j + VW, 6, :], V[:, t - 1, g * HG + j, :],
                                                        pexp[:, (u + j // 2) % 4, j % 2, :],
                                                        start=(t == 1), stop=(t == CT), tile_position=(0, VW * j))
                                    ins.then_inc(s_pv, 1)
                            pe.wait_ge(s_oc, i * NG + g + 1 + 1)
                            pe.wait_ge(s_ou, i * NG + g + 1)
                            for j in range(TB):
                                ins = pe.transpose(ps[:, 4, j * P:j * P + P], oT[:, g % 2, j * P:j * P + P], eye)
                            ins.then_inc(s_ot, 1)

                    with pe.If(ci > 0):
                        attend(True)
                    with pe.Else():
                        attend(False)
                for b in range(B):
                    turn(b)
                    project(b)
                pe.wait_ge(s_res, 2 * B)
                for b in range(B - 1):
                    turn4(b)
                route(0, B - 1, 0)
                route_logits(0, B - 1, 0)

            def fast_way():
                def max_product(b, n):
                    i, place = b % 2, APB * b + n + (n >= A_T0)
                    if n % (AU // 2) == 0:
                        pe.wait_ge(f_rows[i][2 * n // AU], 16 * 7 * (b // 2 + 1))
                    if place >= 2:
                        pe.wait_ge(f_scu, place - 1)
                    h, j = divmod(n, TB)
                    pe.matmul(ps[:, place % 2, :], Q2[0:KR + 1, i, h, j * P:j * P + P], K2[0:KR + 1, i, h, :],
                              start=True, stop=True).then_inc(f_sc, 1)

                def turn_maxima(b, half):
                    place = APB * b + (A_T1 if half else A_T0)
                    pe.wait_ge(f_nm, 2 * b + half + 1)
                    pe.wait_ge(f_scu, place - 1)
                    mt = ps[:, place % 2, 0:256].bitcast(BF16)
                    for j in range(TB):
                        ins = pe.transpose(mt[:, j * P:j * P + P], nmb2[:, j, :, :].rearrange("p t h -> p (t h)"), eye_b[:, :])
                    ins.then_inc(f_sc, 1)

                def max_products(b, lo, hi):
                    for n in range(lo, hi):
                        if n == A_T0:
                            turn_maxima(b, 0)
                        max_product(b, n)

                def turn_values(i):
                    b, g = divmod(i, NG)
                    pe.wait_ge(f_oc, i + 1)
                    if i >= 1:
                        pe.wait_ge(f_ou, i)
                    for j in range(TB):
                        ins = pe.transpose(ps[:, 7, j * P:j * P + P], oT2[:, i % 2, j * P:j * P + P], eye)
                    ins.then_inc(f_ot, 1)

                turn_queries(0)
                queries(0)
                turn_queries(1)
                queries(1)
                pe.wait_ge(f_ones, 16 * 4)
                for j in range(8):
                    if j in (2, 5):
                        share = AU // 8 // KC ** 2
                        queries(2 + j // 5, lambda i: max_products(0, j * AU // 8 + i * share, j * AU // 8 + (i + 1) * share))
                    else:
                        max_products(0, j * AU // 8, (j + 1) * AU // 8)
                    if j in (0, 3):
                        turn_queries(2 + j // 3)
                pe.wait_ge(s_qr, KC * B)
                STEPS_B = NG * CT
                SH = AU // STEPS_B
                for st in range(B * STEPS_B + 1):
                    b, (g, t) = st // STEPS_B, divmod(st % STEPS_B, CT)
                    more = b + 1 < B
                    first = st % STEPS_B * SH
                    if st < B * STEPS_B:
                        if g == 0 and t == 0:
                            if b == 0:
                                turn_maxima(0, 1)
                            pe.wait_ge(f_mr[0], 48 * (b + 1))
                        if g == NG // 2 and t == 0:
                            pe.wait_ge(f_mr[1], 48 * (b + 1))
                        for hp in range(HG // 2):
                            u = 2 * st + hp
                            if u >= 2:
                                pe.wait_ge(f_pe, u - 1)
                            for j in range(2):
                                h = g * HG + hp * 2 + j
                                ins = pe.matmul(ps[:, 2 + 2 * (u % 2) + j, :], K2[0:KROWS, b % 2, h, t * P:t * P + P], Q2[0:KROWS, b % 2, h, :],
                                                start=True, stop=True)
                            ins.then_inc(f_st, 1)
                            if g == 0 and t == 0 and b >= 1 and hp == 0:
                                turn_maxima(b, 1)
                            if more:
                                max_products(b + 1, first + hp, first + hp + 1)
                    if st % CT == 2 and st >= CT:
                        turn_values(st // CT - 1)
                    if st >= 1:
                        i = (st - 1) // CT
                        tv, bv = (st - 1) % CT, (st - 1) // STEPS_B
                        u = 2 * (st - 1)
                        if tv == 0 and i % NG == 0:
                            pe.wait_ge(f_v[bv % 2], 16 * (bv // 2 + 1))
                        pe.wait_ge(f_pe, u + 2)
                        if tv == 0 and i >= 1:
                            pe.wait_ge(f_oc, i)
                        for j in range(HG):
                            ins = pe.matmul(ps[VW * j:VW * j + VW, 6, :], V2[:, bv % 2, tv, i % NG * HG + j, :],
                                            pexp2[:, (u + j // 2) % 4, j % 2, :],
                                            start=(tv == 0), stop=(tv == CT - 1), tile_position=(0, VW * j))
                        ins.then_inc(f_pv, 1)
                    if st < B * STEPS_B and more:
                        max_products(b + 1, first + 2, first + SH)
                    x = st - (B - 1) * STEPS_B
                    if x == 0:
                        pe.wait_ge(f_scu, APB * B)
                    if x in TURN:
                        turn(TURN[x], 0)
                    if x in PROJECT:
                        project(PROJECT[x])
                    if x in TURN4:
                        turn4(TURN4[x], 0)
                    if x == ROUTE:
                        route(0, B - 1, 0)
                    if x == ROUTE + 1:
                        route_logits(0, B - 1, 0)
                turn_values(NG * B - 1)
                pe.wait_ge(f_ou, NG * B)
                turn(B - 1)
                pe.wait_ge(s_l4, 1)
                project(B - 1)

            with pe.If(near > 0):
                general_way()
            tp[0] = tp_before
            with pe.Else():
                fast_way()
            def hidden(b):
                pe.wait_ge(s_pw[b], 16 * 4)
                for f in range(FC):
                    u = b * FC + f
                    if u >= 2:
                        pe.wait_ge(s_p4a, u - 1)
                    for k in range(KC):
                        ins = pe.matmul(ps[:, 4 + u % 2, :], p_w1[:, b, k, f * P:f * P + P], xnT[:, k, S * b:S * b + S],
                                        start=(k == 0), stop=(k == KC - 1))
                    ins.then_inc(s_p4, 1)

            def reasoned(b):
                for m in range(KC):
                    u = b * KC + m
                    pe.wait_ge(s_p4a, FC * (b + 1))
                    if b >= 1:
                        pe.wait_ge(s_rtc, u - 1)
                    for f in range(FC):
                        ins = pe.matmul(ps[:, 2 + m, :], p_w2[:, b, f, m * P:m * P + P], hT[:, b % 2, f, :],
                                        start=(f == 0), stop=(f == FC - 1))
                    ins.then_inc(s_rt, 1)

            def out(b):
                pe.wait_ge(s_rtc, KC * (b + 1))
                if b == 1:
                    pe.wait_ge(s_l4, 2)
                if b >= 2:
                    pe.wait_ge(s_fo, b - 1)
                for t in range(TB):
                    for k in range(KC):
                        ins = pe.matmul(ps[:, 6 * (1 - b % 2) + t // 2, t % 2 * D:t % 2 * D + D], rT[:, b % 2, k, t * P:t * P + P], wof[:, k, :],
                                        start=(k == 0), stop=(k == KC - 1))
                ins.then_inc(s_po, 1)

            hidden(0)
            reasoned(0)
            turn4(B - 1)
            route(B - 1, B, 1)
            hidden(1)
            route_logits(B - 1, B, 1)
            for b in range(1, B):
                if b + 1 < B:
                    hidden(b + 1)
                reasoned(b)
                out(b - 1)
            out(B - 1)

        @block.scalar
        def _(act):
            for s_free in (s_pe, s_wge):
                act.sem_inc(s_free, 1)
            for k in range(B * NF):
                act.wait_ge(s_h, k + 1)
                if k >= 4:
                    act.wait_ge(s_mm2, k - 3)
                act.activation(hid[:, k % 4, :], ps[:, 4 + k % 2, :], ACT.Gelu_apprx_tanh).then_inc(s_a, 1)
            act.wait_ge(s_soft, 1)
            act.activation(t_b[:, :, :], t_a[:, :, :], ACT.Exp).then_inc(s_exp8, 1)
            def last_keys(b):
                for m in range(KC):
                    act.wait_ge(s_ekv, 4 * b + m + 1)
                    if b >= 1:
                        act.wait_ge(s_ekst, 48 * KC * b)
                    act.activation(kp_e[:, 0, m, :], ps[:, 5 * m, :], ACT.Copy).then_inc(s_ek1, 1)
                act.wait_ge(s_evi, b // 2 + 1)
                for m in range(2):
                    act.wait_ge(s_ekv, 4 * b + 3 + m)
                    act.activation(v_e[b // 2][:, b % 2, 2 * m:2 * m + 2, :, 0:DK], ps[:, 5 * m, :].rearrange("p (t h d) -> p t h d", t=2, d=DK),
                                   ACT.Copy).then_inc(s_ev, 1)
            last_keys(0)
            last_keys(1)
            act.wait_ge(s_slot, 2)
            pairs = act.value_load(be_i[0:1, NBLK:NBLK + 1], min_val=1, max_val=PAIRS)
            with act.Fori(0, pairs) as i:
                for j in range(2):
                    act.wait_ge(s_eh, i * 2 + j + 1)
                    act.activation(hexp[:, j, :], ps[:, j, :], ACT.Gelu).then_inc(s_ea, 1)
                for j in range(2):
                    act.wait_ge(s_ey, i * 2 + j + 1)
                    act.wait_ge(s_ys, i * 16 + 1)
                    act.activation(y_s[:, j, :], ps[:, 4 + j, 0:D], ACT.Copy).then_inc(s_eyc, 1)
            act.wait_ge(s_eyc, pairs * 2)
            act.sem_inc(s_expd, 1)
            for b in range(2, B):
                last_keys(b)
            act.wait_ge(s_list, 1)
            near = act.value_load(lst_i[0:1, 33:34], min_val=0, max_val=NC - 1)
            n = act.value_load(lst_i[0:1, 32:33], min_val=1, max_val=B * NC)

            def norm(b, k):
                act.wait_ge(s_lnst, B * k + b + 1)
                for t in range(TB * b, TB * b + TB):
                    ins = act.activation(xn[:, t, :], x_tok[:, t, :], ACT.Identity, bias=nmr_[:, t:t + 1], scale=rstd[:, t:t + 1])
                ins.then_inc(s_ln, 1)

            def query_part(b):
                for m in range(KC):
                    act.wait_ge(s_q, KC * b + m + 1)
                    if b >= 2:
                        act.wait_ge(s_qst[b % 2], 48 * KC * (b // 2))
                    act.activation(qp[:, b % 2, 0, m, :], ps[:, 2 + m, :], ACT.Copy, scale=a128[:, b:b + 1]).then_inc(s_q1, 1)

            def route(lo, hi, i):
                act.wait_ge(s_nv, i + 1)
                act.activation(nav[:, lo:hi], ps[:, 0, 0:hi - lo], ACT.Gelu, bias=bp1[:, 0:1]).then_inc(s_nva, 1)

            def route_exp(lo, hi, i):
                act.wait_ge(s_l4, i + 1)
                act.activation(al[0:hi - lo, i, 2, :], al[0:hi - lo, i, 1, :], ACT.Exp).then_inc(s_e4, 1)

            def general_way():
                for b in range(B):
                    norm(b, 0)
                for b in range(B):
                    query_part(b)
                EPB = CT * H // 2
                with act.Fori(0, n) as i:
                    act.wait_ge(s_kpr, i + 1)
                    act.wait_ge(s_kst, i * (16 * KC) + 1)
                    act.activation(kp[:, 0, :, :], ps[:, 0:KC, :], ACT.Copy).then_inc(s_k1, 1)
                    act.wait_ge(s_vpr, i + 1 + 1)
                    act.wait_ge(s_pv, i * (NG * CT) + 1)
                    act.activation(V[:, :, :, 0:DK], ps[:, 2:4, :].rearrange("p a (t h d) -> p (a t) h d", t=2, d=DK), ACT.Copy).then_inc(s_vt, 1)
                    act.wait_ge(s_wgt, i + 1)
                    act.activation(scl[:, :, :], dif[:, :, :], ACT.Exp).then_inc(s_wge, 1)
                    for u in range(EPB):
                        act.wait_ge(s_st, i * EPB + u + 1)
                        if u >= 4:
                            act.wait_ge(s_pv, i * (NG * CT) + (u - 4) // 2 + 1 + 1)
                        act.activation(pexp[:, u % 4, :, :], ps[:, 2 * (u % 2):2 * (u % 2) + 2, :], ACT.Exp).then_inc(s_pe, 1)
                for b in range(B - 1):
                    norm(b, 1)
                route(0, B - 1, 0)
                route_exp(0, B - 1, 0)

            def take_values(i):
                act.wait_ge(f_pv, CT * (i + 1))
                act.activation(oT2[:, i % 2, :], ps[:, 6, :], ACT.Copy).then_inc(f_oc, 1)

            def take_query_columns(b):
                for k in range(KC):
                    use = TURNS_BEFORE + KC * b + k
                    act.wait_ge(s_tpr, use + 1)
                    act.activation(xnT[:, k, S * b:S * b + S], ps[:, 6 + use % 2, :], ACT.Copy).then_inc(s_tpf, 1)

            def fast_way():
                norm(0, 0)
                take_query_columns(0)
                norm(1, 0)
                query_part(0)
                take_query_columns(1)
                norm(2, 0)
                query_part(1)
                norm(3, 0)
                for b in range(2, B):
                    take_query_columns(b)
                    query_part(b)
                for u in range(B * CT * H // 2):
                    act.wait_ge(f_st, u + 1)
                    if u >= 4:
                        act.wait_ge(f_pv, (u - 4) // 2 + 1)
                    act.activation(pexp2[:, u % 4, :, :], ps[:, 2 + 2 * (u % 2):4 + 2 * (u % 2), :], ACT.Exp).then_inc(f_pe, 1)
                    if u % 2 == 1:
                        st = u // 2
                        if st % CT == 0 and st > 0:
                            take_values(st // CT - 1)
                        x = st - (B - 1) * NG * CT - 2
                        if x in PROJECT:
                            norm(PROJECT[x], 1)
                        if x + 2 == ROUTE:
                            route(0, B - 1, 0)
                        if x + 2 == ROUTE + 2:
                            route_exp(0, B - 1, 0)
                take_values(NG * B - 1)

            with act.If(near > 0):
                general_way()
            with act.Else():
                fast_way()
            for b in range(B):
                act.wait_ge(s_pw[b], 16 * 4)
                for f in range(FC):
                    act.wait_ge(s_p4, b * FC + f + 1)
                    if b >= 2:
                        act.wait_ge(s_rt, KC * (b - 1))
                    act.activation(hT[:, b % 2, f, :], ps[:, 4 + (b * FC + f) % 2, :], ACT.Gelu, bias=p_b1[:, b, f:f + 1]).then_inc(s_p4a, 1)
                if b == 0:
                    norm(B - 1, 1)
                    route(B - 1, B, 1)
                if b == 1:
                    route_exp(B - 1, B, 1)

        @block.vector
        def _(dve):
            ch = Chain(s_dv)
            tp = [0]

            def norm_roots(b):
                lo, hi = TB * b, TB * (b + 1)
                for t in range(lo, hi):
                    ins = dve.bn_stats(stats[:, t, :], x_tok[:, t, :])
                ch.step(dve, ins)
                for t in range(lo, hi):
                    ins = dve.bn_aggr(mv[:, t, :], stats[:, t, :])
                ch.step(dve, ins)
                v, r, q = vare[:, lo:hi], rstd[:, lo:hi], rsq[:, lo:hi]
                ch.step(dve, dve.tensor_scalar(v, mv[:, lo:hi, 1], EPS, None, ALU.add))
                ch.step(dve, dve.tensor_scalar(r.bitcast(I32), v.bitcast(I32), -0.5, float(RSQRT_GUESS), ALU.mult, ALU.add))
                for _ in range(NEWTON):
                    ch.step(dve, dve.tensor_tensor(q, r, r, ALU.mult))
                    ch.step(dve, dve.scalar_tensor_tensor(q, q, -0.5, v, ALU.mult, ALU.mult))
                    ch.step(dve, dve.scalar_tensor_tensor(r, q, 1.5, r, ALU.add, ALU.mult))

            def norm_shifts(b):
                lo, hi = TB * b, TB * (b + 1)
                dve.scalar_tensor_tensor(nmr_[:, lo:hi], mv[:, lo:hi, 0], -1.0, rstd[:, lo:hi], ALU.mult, ALU.mult).then_inc(s_lnst, 1)

            def layer_norm(b):
                norm_roots(b)
                for t in range(TB * b, TB * b + TB):
                    ins = dve.tensor_scalar(xn[:, t, :], x_tok[:, t, :], mv[:, t, 0:1], rstd[:, t:t + 1], ALU.subtract, ALU.mult)
                ins.then_inc(s_ln, 1)

            def take_columns(b, bank=6):
                for k in range(KC):
                    dve.wait_ge(s_tpr, tp[0] + 1)
                    dve.tensor_copy(xnT[:, k, S * b:S * b + S], ps[:, bank + tp[0] % 2, :]).then_inc(s_tpf, 1)
                    tp[0] += 1

            def take_logits(b):
                dve.wait_ge(s_tpr, tp[0] + 1)
                dve.tensor_copy(lg[:, TB * b:TB * b + TB, :].rearrange("p t e -> p (t e)"), ps[:, 6 + tp[0] % 2, 0:TB * E]).then_inc(s_tpf, 1)
                tp[0] += 1

            def query_parts(b):
                for m in range(KC):
                    u = KC * b + m
                    dve.wait_ge(s_q1, u + 1)
                    dve.scalar_tensor_tensor(qr[:, m, :], ps[:, 2 + m, :], a128[:, b:b + 1], qp[:, b % 2, 0, m, :],
                                             ALU.mult, ALU.subtract).then_inc(s_qr, 1)
                    dve.wait_ge(s_qr, u + 1)
                    ch.step(dve, dve.tensor_copy(qp[:, b % 2, 1, m, :], qr[:, m, :]))
                    dve.tensor_tensor(qp[:, b % 2, 2, m, :], qr[:, m, :], qp[:, b % 2, 1, m, :], ALU.subtract).then_inc(s_qp, 1)

            def residual(b, bank):
                for j in range(TB // 2):
                    rows = x_tok[:, TB * b + 2 * j:TB * b + 2 * j + 2, :].rearrange("p t d -> p (t d)")
                    ins = dve.tensor_tensor(rows, rows, ps[:, bank + j, :], ALU.add)
                ins.then_inc(s_res, 1)

            for s_free in (s_scu, s_oc, s_ou):
                dve.sem_inc(s_free, 1)
            dve.memset(zero_t[:, :], 0.0).then_inc(s_zt, 1)
            dve.wait_ge(s_x[0], 16)
            layer_norm(0)
            take_columns(0)
            dve.wait_ge(s_const, 16)
            dve.tensor_copy(eye_b[:, :], cst[:, C_EYE:C_EYE + P])
            dve.tensor_copy(tri_b[:, :], cst[:, C_TRI:C_TRI + P])
            dve.tensor_copy(ones_b[:, :], cst[:, C_ONES:C_ONES + P]).then_inc(s_bconst, 1)
            dve.wait_ge(s_x[1], 16)
            layer_norm(1)
            take_columns(1)
            for b in range(2, 4):
                dve.wait_ge(s_x[b], 16)
                layer_norm(b)
                if b == 2:
                    take_columns(b)
            for b in range(B):
                dve.wait_ge(s_mm2, NF * (b + 1))
                residual(b, b % 2 * 2)
                dve.wait_ge(s_res, b + 1)
                if b == 0:
                    take_columns(3)
                layer_norm(b)
                take_columns(b)
                take_logits(b)
            dve.wait_ge(s_tpf, tp[0])
            ch.step(dve, dve.tensor_reduce(r16[:, :], lg[:, :, :], AX.X, ALU.max))

            def wide(v):
                return v.unsqueeze(2).broadcast_to([P, NT, E])

            def by_expert(v):
                return v.unsqueeze(1).broadcast_to([P, NT, E])

            dve.tensor_tensor(t_a[:, :, :], lg[:, :, :], wide(r16), ALU.subtract).then_inc(s_soft, 1)
            dve.memset(ones8[:, :], 1.0)
            dve.memset(cur[:, :], 0)
            dve.wait_ge(s_exp8, 1)
            ch.step(dve, dve.tensor_reduce(r16[:, :], t_b[:, :, :], AX.X, ALU.add))
            ch.step(dve, dve.reciprocal(gate[:, :], r16[:, :]))
            ch.step(dve, dve.tensor_tensor(pr[:, :, :], t_b[:, :, :], wide(gate), ALU.mult))
            dve.wait_ge(s_cand, 16)
            STEPS = 5
            base = ch.n
            with dve.Fori(0, ROUNDS // 2) as two:
                for j in range(2):
                    r = two * 2 + j
                    c3 = Chain(s_dvr, r * STEPS)
                    c3.step(dve, dve.tensor_tensor(cand[:, :, :], cur.unsqueeze(1).broadcast_to([P, CAND, E]),
                                                   cand_c[:, bass.ds(r * CAND, CAND)].unsqueeze(2).broadcast_to([P, CAND, E]), ALU.bitwise_or))
                    dve.tensor_tensor(ge_b[:, :, :, :],
                                      pr.unsqueeze(1).broadcast_to([P, CAND, NT, E]),
                                      cand.bitcast(F32).unsqueeze(2).broadcast_to([P, CAND, NT, E]), ALU.is_ge).then_inc(s_ge, 1)
                    dve.wait_ge(s_cnt, r + 1)
                    c3.step(dve, dve.tensor_scalar(npass.rearrange("p c e -> p (c e)"), ps[:, 0, 0:CAND * E], CAP - 0.5, None, ALU.is_gt))
                    c3.step(dve, dve.tensor_reduce(nsum[:, :], npass.rearrange("p c e -> p e c"), AX.X, ALU.add))
                    c3.step(dve, dve.tensor_scalar(ninc[:, :], nsum[:, :], cst[:, bass.ds(r + C_STEP, 1)], None, ALU.mult))
                    c3.step(dve, dve.tensor_tensor(cur[:, :], cur[:, :], ninc[:, :], ALU.bitwise_or))
            thr = cur.bitcast(F32)
            dve.tensor_tensor(gt[:, :, :], pr[:, :, :], by_expert(thr), ALU.is_gt)
            dve.tensor_tensor(eq_b[:, :, :], pr[:, :, :], by_expert(thr), ALU.is_equal).then_inc(s_gq, 1)
            dve.wait_ge(s_gp, 1)
            ch.step(dve, dve.tensor_scalar(need[:, :], ps[:, 2, 0:E], -1.0, float(CAP), ALU.mult, ALU.add))
            ch.step(dve, dve.tensor_tensor(t_a[:, :, :], ps[:, 1, 0:NT * E].rearrange("p (t e) -> p t e", e=E), by_expert(need), ALU.is_lt))
            ch.step(dve, dve.tensor_tensor(t_a[:, :, :], t_a[:, :, :], eq_b[:, :, :], ALU.mult))
            ch.step(dve, dve.tensor_tensor(sel[:, :, :], t_a[:, :, :], gt[:, :, :], ALU.add))
            ch.step(dve, dve.tensor_reduce(asg[:, :], sel[:, :, :], AX.X, ALU.max))
            ch.step(dve, dve.tensor_tensor(t_a[:, :, :], wide(asg), sel[:, :, :], ALU.subtract))
            ch.step(dve, dve.scalar_tensor_tensor(t_b[:, :, :], t_a[:, :, :], -2.0, pr[:, :, :], ALU.mult, ALU.add))
            ch.step(dve, dve.tensor_reduce(gate[:, :], t_b[:, :, :], AX.X, ALU.max))
            ch.step(dve, dve.tensor_tensor(t_a[:, :, :], t_b[:, :, :], wide(gate), ALU.is_equal))
            ch.step(dve, dve.tensor_tensor(t_a[:, :, :], t_a[:, :, :], by_expert(cst[:, C_EM8:C_EM8 + E]), ALU.mult))
            ch.step(dve, dve.tensor_reduce(r16[:, :], t_a[:, :, :], AX.X, ALU.min))
            dve.tensor_tensor(hot_b[:, :, :], by_expert(cst[:, C_EM8:C_EM8 + E]), wide(r16), ALU.is_equal).then_inc(s_gq, 1)
            dve.wait_ge(s_gp, 2)
            ch.step(dve, dve.tensor_tensor(nbw[:, :, :], ps[:, 4, 0:E].unsqueeze(2).broadcast_to([P, E, NT]),
                                           cst[:, C_JT:C_JT + NT].unsqueeze(1).broadcast_to([P, E, NT]), ALU.is_gt))
            ch.step(dve, dve.tensor_reduce(nb[:, :], nbw[:, :, :], AX.X, ALU.add))
            ch.step(dve, dve.tensor_tensor_scan(cb[:, :], ones8[:, :], nb[:, :], 0.0, ALU.mult, ALU.add))
            ch.step(dve, dve.tensor_tensor(base_s[:, :], cb[:, :], nb[:, :], ALU.subtract))
            ch.step(dve, dve.scalar_tensor_tensor(t_a[:, :, :], by_expert(base_s), float(P), ps[:, 3, 0:NT * E].rearrange("p (t e) -> p t e", e=E),
                                                  ALU.mult, ALU.add))
            dve.wait_ge(s_gq, 2)
            ch.step(dve, dve.tensor_tensor(t_a[:, :, :], t_a[:, :, :], hot_b[:, :, :], ALU.mult))
            ch.step(dve, dve.tensor_reduce(r16[:, :], t_a[:, :, :], AX.X, ALU.add))
            dve.tensor_copy(slot_i[:, :], r16[:, :]).then_inc(s_slot, 1)
            ch.step(dve, dve.tensor_tensor(be_w[:, :, :], cb.unsqueeze(1).broadcast_to([P, NBLK, E]),
                                           cst[:, C_JB:C_JB + NBLK].unsqueeze(2).broadcast_to([P, NBLK, E]), ALU.is_le))
            ch.step(dve, dve.tensor_reduce(be[:, :], be_w[:, :, :], AX.X, ALU.add))
            dve.tensor_scalar(be_i[:, 0:NBLK], be[:, :], float(E - 1), float(KC * F), ALU.min, ALU.mult)
            ch.step(dve, dve.tensor_scalar(pw[:, :], cst[:, C_JB:C_JB + NBLK:2], cb[:, E - 1:E], None, ALU.is_lt))
            ch.step(dve, dve.tensor_reduce(need[:, 0:1], pw[:, :], AX.X, ALU.add))
            dve.tensor_copy(be_i[:, NBLK:NBLK + 1], need[:, 0:1]).then_inc(s_slot, 1)
            def set_values(i):
                dve.memset(v_e[i][:, :, :, :, DK + 1:], 0.0)
                dve.memset(v_e[i][:, :, :, :, DK:DK + 1], 1.0).then_inc(s_evi, 1)

            def last_keys(b):
                for m in range(KC):
                    dve.wait_ge(s_ek1, KC * b + m + 1)
                    dve.tensor_tensor(kr_e[:, m, :], ps[:, 5 * m, :], kp_e[:, 0, m, :], ALU.subtract).then_inc(s_ekr, 1)
                    dve.wait_ge(s_ekr, KC * b + m + 1)
                    ch.step(dve, dve.tensor_copy(kp_e[:, 1, m, :], kr_e[:, m, :]))
                    dve.tensor_tensor(kp_e[:, 2, m, :], kr_e[:, m, :], kp_e[:, 1, m, :], ALU.subtract).then_inc(s_ekp, 1)

            dve.wait_ge(s_mask, 48)
            ch.step(dve, dve.tensor_copy(maskw[:, 1, :], mask4[:, :].bitcast(U8)))
            dve.tensor_reduce(msm[:, 0:1], maskw[:, 1, :], AX.X, ALU.max).then_inc(s_mk, 1)
            dve.wait_ge(s_mkp, 1)
            dve.tensor_scalar(a128[:, :], ps[:, 7, 0:B], 1.0, None, ALU.min)
            ch.step(dve, dve.tensor_scalar(msm[:, 1:2], ps[0:B * NC, 6, 0:1], 1.0, None, ALU.min))
            ch.step(dve, dve.tensor_scalar(msm[:, 2:3], msm[:, 1:2], -1.0, 1.0, ALU.mult, ALU.add))
            dve.wait_ge(s_mk, 1)
            dve.tensor_tensor(msm[:, 3:4], msm[:, 2:3], msm[:, 0:1], ALU.max).then_inc(s_mk2, 1)
            ch.step(dve, dve.scalar_tensor_tensor(maskw[:, 2, :], maskw[:, 0, :], msm[:, 2:3], maskw[:, 1, :], ALU.mult, ALU.max))
            dve.tensor_scalar(mrow_b[:, :], maskw[:, 2, :], 1.0, -NEG, ALU.subtract, ALU.mult).then_inc(s_mrow, 1)
            set_values(0)
            last_keys(0)
            dve.wait_ge(s_lrow, 1)
            ch.step(dve, dve.tensor_copy(lst[:, 0, :], ps[0:1, 6, 0:16]))
            ch.step(dve, dve.tensor_tensor_scan(lst[:, 1, :], cst[0:1, C_ONES:C_ONES + 16], lst[:, 0, :], 0.0, ALU.mult, ALU.add))
            ch.step(dve, dve.tensor_tensor(lst2[:, :, :], lst[:, 1, :].unsqueeze(1).broadcast_to([1, 16, 16]),
                                           cst[0:1, C_LIST + 32:C_LIST + 48].unsqueeze(2).broadcast_to([1, 16, 16]), ALU.is_equal))
            ch.step(dve, dve.tensor_tensor(lst2[:, :, :], lst2[:, :, :], lst[:, 0, :].unsqueeze(1).broadcast_to([1, 16, 16]), ALU.mult))
            for q in range(2):
                ch.step(dve, dve.tensor_tensor(lst3[:, :, :], lst2[:, :, :],
                                               cst[0:1, C_LIST + 16 * q:C_LIST + 16 * q + 16].unsqueeze(1).broadcast_to([1, 16, 16]), ALU.mult))
                ch.step(dve, dve.tensor_reduce(lst[:, 2 + q, :], lst3[:, :, :], AX.X, ALU.add))
                dve.tensor_copy(lst_i[:, 16 * q:16 * q + 16], lst[:, 2 + q, :])
            ch.step(dve, dve.tensor_tensor(lst[:, 4, :], lst[:, 0, :], cst[0:1, C_LIST + 16:C_LIST + 32], ALU.mult))
            ch.step(dve, dve.tensor_reduce(lst[:, 5, 0:1], lst[:, 4, :], AX.X, ALU.max))
            dve.tensor_copy(lst_i[:, 33:34], lst[:, 5, 0:1])
            dve.tensor_copy(lst_i[:, 32:33], lst[:, 1, 15:16]).then_inc(s_list, 1)
            last_keys(1)
            for j in range(2):
                dve.wait_ge(s_xsTr, j + 1)
                dve.tensor_copy(xsT[:, j, :, :].rearrange("p k n -> p (k n)"), ps[:, 6 + j, 0:KC * P]).then_inc(s_xsT, 1)
            pairs = dve.value_load(be_i[0:1, NBLK:NBLK + 1], min_val=1, max_val=PAIRS)
            with dve.Fori(0, pairs) as i:
                for j in range(2):
                    dve.wait_ge(s_et, i * 2 + j + 1)
                    dve.tensor_copy(hexpT[:, j, :, :].rearrange("p k n -> p (k n)"), ps[:, 2 + j, :]).then_inc(s_etc, 1)
                for j in range(2):
                    dve.wait_ge(s_xsTr, i * 2 + j + 3)
                    dve.tensor_copy(xsT[:, j, :, :].rearrange("p k n -> p (k n)"), ps[:, 6 + j, 0:KC * P]).then_inc(s_xsT, 1)
            dve.wait_ge(s_expd, 1)
            set_values(1)
            for b in range(2, B):
                last_keys(b)
            def add_experts(b):
                dve.wait_ge(s_gat[b], 16 * TB)
                for t in range(TB * b, TB * b + TB):
                    ins = dve.scalar_tensor_tensor(x_tok[:, t, :], yg[:, t, :], gate[:, t:t + 1], x_tok[:, t, :], ALU.mult, ALU.add)
                ins.then_inc(s_moe, 1)
                dve.wait_ge(s_moe, b + 1)
                norm_roots(b)
                norm_shifts(b)

            near = dve.value_load(lst_i[0:1, 33:34], min_val=0, max_val=NC - 1)

            def project(b):
                dve.wait_ge(s_pj, b + 1)
                residual(b, 0)
                dve.wait_ge(s_res, B + b + 1)
                norm_roots(b)
                norm_shifts(b)

            steps_before, tp_before = ch.n, tp[0]

            def route_shift(lo, hi, i):
                n = hi - lo
                dve.wait_ge(s_nl, i + 1)
                dve.wait_ge(s_w4, 16 * 6)
                ch.step(dve, dve.tensor_tensor(al[0:n, i, 0, :], ps[0:n, 1, 0:E], bp2[0:n, :], ALU.add))
                ch.step(dve, dve.tensor_reduce(al[0:n, i, 7, 0:1], al[0:n, i, 0, :], AX.X, ALU.max))
                dve.tensor_scalar(al[0:n, i, 1, :], al[0:n, i, 0, :], al[0:n, i, 7, 0:1], None, ALU.subtract).then_inc(s_l4, 1)

            def choose(lo, hi, i):
                n = hi - lo
                dve.wait_ge(s_e4, i + 1)
                ch.step(dve, dve.tensor_reduce(al[0:n, i, 7, 1:2], al[0:n, i, 2, :], AX.X, ALU.add))
                ch.step(dve, dve.reciprocal(al[0:n, i, 7, 4:5], al[0:n, i, 7, 1:2]))
                ch.step(dve, dve.tensor_scalar(al[0:n, i, 3, :], al[0:n, i, 2, :], al[0:n, i, 7, 4:5], None, ALU.mult))
                ch.step(dve, dve.tensor_reduce(al[0:n, i, 7, 2:3], al[0:n, i, 3, :], AX.X, ALU.max))
                ch.step(dve, dve.tensor_scalar(al[0:n, i, 4, :], al[0:n, i, 3, :], al[0:n, i, 7, 2:3], None, ALU.is_equal))
                ch.step(dve, dve.tensor_tensor(al[0:n, i, 5, :], al[0:n, i, 4, :], cst[0:n, C_EM8:C_EM8 + E], ALU.mult))
                ch.step(dve, dve.tensor_reduce(al[0:n, i, 7, 3:4], al[0:n, i, 5, :], AX.X, ALU.min))
                dve.tensor_scalar(sel_i[0:n, i:i + 1], al[0:n, i, 7, 3:4], float(E), None, ALU.add).then_inc(s_sel, 1)

            def base(b):
                rows = slice(TB * b, TB * b + TB)
                dve.wait_ge(s_ln, 3 * B + b + 1)
                ch.step(dve, dve.tensor_tensor(o_s[:, rows, :], xn[:, rows, :], bo_s.unsqueeze(1).broadcast_to([P, TB, D]), ALU.add))
                ch.step(dve, dve.tensor_tensor(o_s[:, rows, :], o_s[:, rows, :], x_tok[:, rows, :], ALU.add))

            def general_way():
                for b in range(B):
                    add_experts(b)
                for b in range(B):
                    take_columns(b)
                    query_parts(b)
                for i in range(2):
                    dve.wait_ge(s_qst[i], 48 * KC * B // 2)
                dve.memset(nmb[:, :, :, :], 0.0)
                dve.memset(V[:, :, :, :], 0.0)
                dve.memset(acc[:, :, :, :, :], 0.0)
                dve.memset(m_run[:, :, :], NEG).then_inc(s_init3, 1)
                for j in range(NY // 512):
                    dve.wait_ge(s_dp, j + 1)
                    dve.tensor_copy(dist_s[0:H, j * 512:j * 512 + 512], ps[0:H, 3 + j, :]).then_inc(s_dpc, 1)
                dve.wait_ge(s_dpc, NY // 512)
                for b in range(B):
                    if b >= 1:
                        dve.wait_ge(s_dstore, 16 * b)
                    dve.tensor_scalar(dist_g[0:H, :], dist_s[0:H, :], a128[0:H, b:b + 1], None, ALU.mult).then_inc(s_dst, 1)
                dve.wait_ge(s_dstore, 16 * B)
                dve.memset(Q[KR:KROWS, :, :], 1.0)
                dve.memset(K[KR:KROWS, :, :], 1.0)
                dve.memset(V[:, :, :, DK:DK + 1], 1.0).then_inc(s_rows, 1)
                n = dve.value_load(lst_i[0:1, 32:33], min_val=1, max_val=B * NC)
                SPB = H * TB // 2
                STEPS3 = 9
                with dve.Fori(0, n) as i:
                    c3 = Chain(s_dv3, i * STEPS3)
                    bi = dve.value_load(lst_i[0:1, bass.ds(i, 1)], min_val=0, max_val=B - 1)
                    dve.wait_ge(s_k1, i + 1)
                    c3.step(dve, dve.tensor_tensor(kf[:, :, :], ps[:, 0:KC, :], kp[:, 0, :, :], ALU.subtract))
                    c3.step(dve, dve.tensor_copy(kp[:, 1, :, :], kf[:, :, :]))
                    dve.tensor_tensor(kp[:, 2, :, :], kf[:, :, :], kp[:, 1, :, :], ALU.subtract).then_inc(s_kp, 1)
                    for u in range(SPB):
                        h, jp = divmod(u, TB // 2)
                        dve.wait_ge(s_sc, i * SPB + u + 1)
                        dve.tensor_reduce(cmax[:, h, 2 * jp:2 * jp + 2], ps[:, 2 * (u % 2):2 * (u % 2) + 2, :], AX.X, ALU.max).then_inc(s_scu, 1)
                    dve.wait_ge(s_scu, (i + 1) * SPB + 1)
                    c3.step(dve, dve.tensor_scalar(nm[:, :, :], cmax[:, :, :], -1.0, None, ALU.mult))
                    nmv = nm.rearrange("p h j -> p j h")
                    rv = nmr.rearrange("p h j -> p j h")
                    c3.step(dve, dve.tensor_copy(nmb[:, :, 0, :], nmv))
                    c3.step(dve, dve.tensor_tensor(rv, nmv, nmb[:, :, 0, :], ALU.subtract))
                    c3.step(dve, dve.tensor_copy(nmb[:, :, 1, :], rv))
                    dve.tensor_tensor(nmb[:, :, 2, :], rv, nmb[:, :, 1, :], ALU.subtract).then_inc(s_nm, 1)
                    cm = cmax.rearrange("p h j -> p (h j)")
                    run = m_run[:, bass.ds(bi, 1), :].rearrange("p b c -> p (b c)")
                    c3.step(dve, dve.tensor_tensor(m_new[:, :], run, cm, ALU.max))
                    dve.wait_ge(s_wge, i + 1)
                    dve.tensor_tensor(dif[:, 0, :], run, m_new[:, :], ALU.subtract)
                    c3.step(dve, dve.tensor_tensor(dif[:, 1, :], cm, m_new[:, :], ALU.subtract))
                    c3.step(dve, dve.tensor_tensor(run, m_new[:, :], m_new[:, :], ALU.max))
                    dve.tensor_copy(m_new[:, 0:1], m_new[:, 0:1]).then_inc(s_wgt, 1)
                    dve.wait_ge(s_nmt, i + 1)
                    dve.wait_ge(s_mr, i * 48 + 1)
                    dve.tensor_copy(mrow[0:3 * H, :], ps[0:3 * H, 7, 0:256].bitcast(BF16)).then_inc(s_nmc, 1)
                    for g in range(NG):
                        dve.wait_ge(s_pv, i * (NG * CT) + (g + 1) * CT + 1)
                        dve.tensor_copy(oT[:, g % 2, :], ps[:, 6, :]).then_inc(s_oc, 1)
                        if g == 0:
                            dve.wait_ge(s_wge, i + 1 + 1)

                        def weight(w):
                            return (scl[:, w, g * HG * TB:(g + 1) * HG * TB].rearrange("p (h j) -> p j h", j=TB)
                                    .unsqueeze(3).broadcast_to([P, TB, HG, DK + 1]))

                        av = acc[:, bass.ds(bi, 1), :, g * HG:(g + 1) * HG, :].rearrange("p b j h d -> p (b j) h d")
                        dve.tensor_tensor(av, av, weight(0), ALU.mult)
                        dve.wait_ge(s_ot, i * NG + g + 1)
                        dve.tensor_tensor(tmp[:, :, :, :], ps[:, 4, :].rearrange("p (j h v) -> p j h v", j=TB, h=HG)[:, :, :, 0:DK + 1],
                                          weight(1), ALU.mult).then_inc(s_dvm, 1)
                        dve.wait_ge(s_dvm, i * NG + g + 1)
                        dve.tensor_tensor(av, av, tmp[:, :, :, :], ALU.add).then_inc(s_ou, 1)
                dve.wait_ge(s_ou, n * NG + 1)
                accv = acc.rearrange("p b j h d -> p (b j) h d")
                Chain(f_dv).step(dve, dve.reciprocal(rl.unsqueeze(3), accv[:, :, :, DK:DK + 1]))
                for b in range(B):
                    dve.tensor_tensor(xn[:, TB * b:TB * b + TB, :].rearrange("p t (h d) -> p t h d", d=DK),
                                      accv[:, TB * b:TB * b + TB, :, 0:DK],
                                      rl[:, TB * b:TB * b + TB, :].unsqueeze(3).broadcast_to([P, TB, H, DK]), ALU.mult).then_inc(s_acc_f, 1)
                for b in range(B):
                    take_columns(b)
                    project(b)
                for b in range(B - 1):
                    take_columns(b)
                route_shift(0, B - 1, 0)
                choose(0, B - 1, 0)

            def fast_way():
                cf = Chain(f_dv)
                assert tp[0] == TURNS_BEFORE
                tp[0] += KC * B
                add_experts(0)
                add_experts(1)
                add_experts(2)
                query_parts(0)
                add_experts(3)
                query_parts(1)
                dve.memset(nmb2[:, :, :, :], 0.0)

                def maxima(b, n):
                    place = APB * b + n + (n >= A_T0)
                    h, j = divmod(n, TB)
                    dve.wait_ge(f_sc, place + 1)
                    dve.tensor_reduce(cmax2[:, h, j:j + 1], ps[:, place % 2, :], AX.X, ALU.max).then_inc(f_scu, 1)

                def split_maxima(b, half):
                    dve.wait_ge(f_scu, APB * b + (AU // 2 if half == 0 else A_T1))
                    cf.step(dve, dve.tensor_scalar(nm2[:, :, :], cmax2[:, half * HH:half * HH + HH, :], -1.0, None, ALU.mult))
                    nv, rv = nm2.rearrange("p h j -> p j h"), nr2.rearrange("p h j -> p j h")
                    cf.step(dve, dve.tensor_copy(nmb2[:, :, 0, :], nv))
                    cf.step(dve, dve.tensor_tensor(rv, nv, nmb2[:, :, 0, :], ALU.subtract))
                    cf.step(dve, dve.tensor_copy(nmb2[:, :, 1, :], rv))
                    dve.tensor_tensor(nmb2[:, :, 2, :], rv, nmb2[:, :, 1, :], ALU.subtract).then_inc(f_nm, 1)

                def take_maxima(b, half):
                    place = APB * b + (A_T1 if half else A_T0)
                    if b >= 1:
                        dve.wait_ge(f_mr[half], 48 * b)
                    dve.wait_ge(f_sc, place + 1)
                    dve.tensor_copy(mrow2[0:3 * HH, half, :], ps[0:3 * HH, place % 2, 0:256].bitcast(BF16)).then_inc(f_scu, 1)

                def max_steps(b, lo, hi):
                    for n in range(lo, hi):
                        if n == AU // 2:
                            split_maxima(b, 0)
                        if n == A_T0:
                            take_maxima(b, 0)
                        maxima(b, n)
                    if hi == AU:
                        split_maxima(b, 1)

                def normalise(i):
                    b, g = divmod(i, NG)
                    dve.wait_ge(f_ot, i + 1)
                    v = ps[:, 7, :].rearrange("p (j h v) -> p j h v", j=TB, h=HG)
                    cf.step(dve, dve.reciprocal(rl2[:, :, :, :], v[:, :, :, DK:DK + 1]))
                    ins = dve.tensor_tensor(xn[:, TB * b:TB * b + TB, g * HG * DK:(g + 1) * HG * DK].rearrange("p t (h d) -> p t h d", d=DK),
                                            v[:, :, :, 0:DK], rl2.broadcast_to([P, TB, HG, DK]), ALU.mult)
                    ins.then_inc(f_ou, 1)
                    if g == NG - 1:
                        dve.wait_ge(f_ou, i + 1)
                        dve.sem_inc(s_acc_f, 1)

                for j in range(8):
                    max_steps(0, j * AU // 8, (j + 1) * AU // 8)
                    if j in (3, 6):
                        query_parts(2 + j // 6)
                STEPS_B = NG * CT
                SH = AU // STEPS_B
                for st in range(B * STEPS_B):
                    b = st // STEPS_B
                    if st % STEPS_B == 0:
                        take_maxima(b, 1)
                    if b + 1 < B:
                        max_steps(b + 1, st % STEPS_B * SH, (st % STEPS_B + 1) * SH)
                    if st % CT == 2 and st >= CT:
                        normalise(st // CT - 1)
                    x = st - (B - 1) * STEPS_B
                    if x in TURN:
                        take_columns(TURN[x], 0)
                    if x in PROJECT:
                        project(PROJECT[x])
                    if x in TURN4:
                        take_columns(TURN4[x], 0)
                    if x == ROUTE + 1:
                        route_shift(0, B - 1, 0)
                choose(0, B - 1, 0)
                normalise(NG * B - 1)
                take_columns(B - 1)
                project(B - 1)

            with dve.If(near > 0):
                general_way()
            ch.n, tp[0] = steps_before, tp_before
            with dve.Else():
                fast_way()
            ch.step(dve, dve.tensor_scalar(bo_s[:, :], bo_s[:, :], 0.3, None, ALU.mult))

            def answers(b):
                if b >= 2:
                    dve.wait_ge(s_po, b - 1)
                for m in range(KC):
                    dve.wait_ge(s_rt, KC * b + m + 1)
                    dve.tensor_scalar(rT[:, b % 2, m, :], ps[:, 2 + m, :], p_b2[:, b, m:m + 1], None, ALU.add).then_inc(s_rtc, 1)

            base(0)
            answers(0)
            take_columns(B - 1)
            route_shift(B - 1, B, 1)
            choose(B - 1, B, 1)
            for b in range(B):
                if b + 1 < B:
                    answers(b + 1)
                    base(b + 1)
                dve.wait_ge(s_po, b + 1)
                for j in range(TB // 2):
                    rows = o_s[:, TB * b + 2 * j:TB * b + 2 * j + 2, :].rearrange("p t d -> p (t d)")
                    ins = dve.scalar_tensor_tensor(rows, ps[:, 6 * (1 - b % 2) + j, :], 0.3, rows, ALU.mult, ALU.add)
                ins.then_inc(s_fo, 1)

        @block.gpsimd
        def _(pool):
            pool.wait_ge(s_slot, 2)
            pool.wait_ge(s_ln, 2 * B)
            pool.wait_ge(s_zero, 32)
            for t in range(NT):
                pool.indirect_dma_start(xs_d, bass.IndirectOffsetOnAxis(ap=slot_i[:, t:t + 1].bitcast(U32), axis=0),
                                        xn[:, t, :], None).then_inc(s_scat, 16)
            pool.wait_ge(s_ysd, 1)
            for i in range(2):
                pool.wait_ge(s_evst[i], 16)
            for t in range(NT):
                pool.indirect_dma_start(yg[:, t, :], None, ys_d,
                                        bass.IndirectOffsetOnAxis(ap=slot_i[:, t:t + 1].bitcast(U32), axis=0)).then_inc(s_gat[t // TB], 16)


NAMES = {
    "x": [T, D], "ctxT": [B, D, LP], "ctxN": [B, NF * P, D], "mask": [B * NC, CH // 4], "Wg": [D, E], "W1": [E, D, F], "W2": [E, F, D],
    "WqT": [D, D], "WkT": [D, D], "WvT": [D, D], "WoT": [D, D], "rel_biasT": [BUCKETS, H], "Wp1": [D, NAV], "bp1": [NAV],
    "Wp2": [NAV, E], "bp2": [E], "pW1": [E, D, F], "pb1": [E, F], "pW2": [E, F, D], "pb2": [E, D], "Wof": [D, D], "bo": [D],
}


def lay_out(x, ctx_1024, mask_Bx1x1xS2_bk0, L0_ffn_Wg, L0_ffn_W1, L0_ffn_W2, L1_xattn_Wq, L1_xattn_Wk, L1_xattn_Wv, L1_xattn_Wo,
            L1_xattn_rel_bias, L1_ffn_Wp1, L1_ffn_bp1, L1_ffn_Wp2, L1_ffn_bp2, L1_ffn_W1, L1_ffn_b1, L1_ffn_W2, L1_ffn_b2, L1_ffn_Wo, L1_ffn_bo):
    c = np.asarray(ctx_1024)[:, ::-1, :]
    ctxT = np.zeros((B, D, LP), np.float32)
    ctxT[:, :, 0:L] = c.transpose(0, 2, 1)
    ctxN = np.zeros((B, NF * P, D), np.float32)
    ctxN[:, 0:L, :] = c
    mask = np.zeros((B, LP), np.uint8)
    mask[:, 0:L] = np.asarray(mask_Bx1x1xS2_bk0).reshape(B, L)[:, ::-1].view(np.uint8)
    arrays = {
        "x": np.asarray(x).reshape(T, D), "ctxT": ctxT, "ctxN": ctxN, "mask": mask.reshape(B * NC, CH).view(np.int32),
        "Wg": L0_ffn_Wg, "W1": L0_ffn_W1, "W2": L0_ffn_W2,
        "WqT": np.asarray(L1_xattn_Wq).T, "WkT": np.asarray(L1_xattn_Wk).T, "WvT": np.asarray(L1_xattn_Wv).T,
        "WoT": np.asarray(L1_xattn_Wo).T, "rel_biasT": np.asarray(L1_xattn_rel_bias).T,
        "Wp1": L1_ffn_Wp1, "bp1": L1_ffn_bp1, "Wp2": L1_ffn_Wp2, "bp2": L1_ffn_bp2, "pW1": L1_ffn_W1, "pb1": L1_ffn_b1,
        "pW2": L1_ffn_W2, "pb2": L1_ffn_b2, "Wof": L1_ffn_Wo, "bo": L1_ffn_bo,
    }
    arrays = {k: np.ascontiguousarray(np.asarray(v)) for k, v in arrays.items()}
    arrays.update(shape_constants())
    return arrays


def program(nc):
    shapes = {k: (v, I32 if k == "mask" else F32) for k, v in NAMES.items()}
    for k, v in shape_constants().items():
        shapes[k] = (list(v.shape), mybir.dt.from_np(v.dtype))
    a = {k: nc.dram_tensor(f"in_{k}", s, dt, kind="ExternalInput").ap() for k, (s, dt) in shapes.items()}
    a["out"] = nc.dram_tensor("out_0", [T, D], F32, kind="ExternalOutput").ap()
    build(nc, a)


def kernel(**inputs):
    import concourse.bacc as bacc
    from concourse.bass_utils import run_bass_kernel_spmd
    nc = bacc.Bacc("TRN2", target_bir_lowering=False, num_devices=1)
    program(nc)
    arrays = {f"in_{k}": v for k, v in lay_out(**inputs).items()}
    r = run_bass_kernel_spmd(nc, [arrays], core_ids=[0])
    return r.results[0]["out_0"].reshape(B, S, D)
```
